# Optimizing a Trainium2 kernel written in Bass

```python
import numpy as np
import jax
import jax.numpy as jnp

def _softmax(x, axis=-1):
    return jax.nn.softmax(x, axis=axis)

def _gelu(x):
    return jax.nn.gelu(x, approximate=True)

def _silu(x):
    return jax.nn.silu(x)

def _sigmoid(x):
    return jax.nn.sigmoid(x)

def _layernorm(x, axis=-1, eps=1e-05):
    m = jnp.mean(x, axis=axis, keepdims=True)
    v = jnp.var(x, axis=axis, keepdims=True)
    return (x - m) / jnp.sqrt(v + eps)

def _scatter_add(tgt, idx, src, axis=0):
    return tgt.at[idx].add(src)

def _segment_sum(src, seg, n):
    return jax.ops.segment_sum(src, seg, n)
kernel_name = 'mk_sandwich_d1_jaxref_r8_e04fa8'

def setup_inputs(seed: int=0):
    np.random.seed(seed)
    _w = jnp.asarray

    def _L0_attn_setup():
        import jax, jax.numpy as jnp
        import numpy as np
        DIM = 256
        HIDDEN = 256
        HEADS = 4
        HD = HIDDEN // HEADS
        EPS = 1e-06
        BATCH = 4
        SEQ = 256
        key = jax.random.key(seed)
        k0, k1, k2, k3 = jax.random.split(key, 4)
        s = 0.02
        x = jax.random.normal(k0, (BATCH, SEQ, DIM), dtype=jnp.float32)
        W_in = jax.random.normal(k1, (HIDDEN, DIM), dtype=jnp.float32) * s
        W_gate = jax.random.normal(k2, (4 * HIDDEN, HIDDEN), dtype=jnp.float32) * s
        b_gate = jnp.zeros((4 * HIDDEN,), dtype=jnp.float32)
        rms_w = jnp.ones((HD,), dtype=jnp.float32)
        W_out = jax.random.normal(k3, (DIM, HIDDEN), dtype=jnp.float32) * s
        return {'x': x, 'W_in': W_in, 'W_gate': W_gate, 'b_gate': b_gate, 'rms_w': rms_w, 'W_out': W_out}
    _L0_attn_in = _L0_attn_setup()

    def _L0_ffn_setup():
        import jax, jax.numpy as jnp
        import numpy as np
        ALPHA = 1.702
        LIMIT = 7.0
        TOP_K = 4
        B, S, H = (1, 128, 256)
        E, D = (16, 256)
        key = jax.random.key(seed)
        ks = jax.random.split(key, 7)
        s = 0.02
        return {'hidden_states': jax.random.normal(ks[0], (B, S, H), dtype=jnp.float32), 'router_weight': jax.random.normal(ks[1], (E, H), dtype=jnp.float32) * s, 'router_bias': jax.random.normal(ks[2], (E,), dtype=jnp.float32) * s, 'gate_up_proj': jax.random.normal(ks[3], (E, H, 2 * D), dtype=jnp.float32) * s, 'gate_up_proj_bias': jax.random.normal(ks[4], (E, 2 * D), dtype=jnp.float32) * s, 'down_proj': jax.random.normal(ks[5], (E, D, H), dtype=jnp.float32) * s, 'down_proj_bias': jax.random.normal(ks[6], (E, H), dtype=jnp.float32) * s}
    _L0_ffn_in = _L0_ffn_setup()
    _d = {'L0_attn_x': _L0_attn_in['x'], 'L0_attn_W_in': _L0_attn_in['W_in'], 'L0_attn_W_gate': _L0_attn_in['W_gate'], 'L0_attn_b_gate': _L0_attn_in['b_gate'], 'L0_attn_rms_w': _L0_attn_in['rms_w'], 'L0_attn_W_out': _L0_attn_in['W_out'], 'L0_ffn_router_weight': _L0_ffn_in['router_weight'], 'L0_ffn_router_bias': _L0_ffn_in['router_bias'], 'L0_ffn_gate_up_proj': _L0_ffn_in['gate_up_proj'], 'L0_ffn_gate_up_proj_bias': _L0_ffn_in['gate_up_proj_bias'], 'L0_ffn_down_proj': _L0_ffn_in['down_proj'], 'L0_ffn_down_proj_bias': _L0_ffn_in['down_proj_bias']}
    _x0 = _d['L0_attn_x']
    _d['L0_attn_x'] = jax.random.normal(jax.random.fold_in(jax.random.key(seed), 1), (16, 256, 256), dtype=_x0.dtype)
    del _x0
    return _d

def reference(L0_attn_x, L0_attn_W_in, L0_attn_W_gate, L0_attn_b_gate, L0_attn_rms_w, L0_attn_W_out, L0_ffn_router_weight, L0_ffn_router_bias, L0_ffn_gate_up_proj, L0_ffn_gate_up_proj_bias, L0_ffn_down_proj, L0_ffn_down_proj_bias):

    def _L0_attn_ref(x, W_in, W_gate, b_gate, rms_w, W_out):
        import jax, jax.numpy as jnp
        import numpy as np
        DIM = 256
        HIDDEN = 256
        HEADS = 4
        HD = HIDDEN // HEADS
        EPS = 1e-06
        BATCH = 4
        SEQ = 256
        B, L, _ = x.shape
        xp = x @ W_in.T
        gates = xp @ W_gate.T + b_gate
        gates = gates.reshape(B, L, HEADS, 4 * HD).transpose(0, 2, 1, 3)
        i_g, f_g, o_g, c_t = jnp.split(gates, 4, axis=-1)
        i_g = jnp.exp(i_g)
        f_g = jax.nn.sigmoid(f_g)
        o_g = jax.nn.sigmoid(o_g)
        c_t = jnp.tanh(c_t)
        tm = lambda a: jnp.moveaxis(a, 2, 0)

        def step(c, g):
            i, f, o, cd = g
            c = f * c + i * cd
            c_norm = c * jax.lax.rsqrt(jnp.mean(c * c, axis=-1, keepdims=True) + EPS) * rms_w
            h = o * jnp.tanh(c_norm)
            return (c, h)
        c0 = jnp.zeros((B, HEADS, HD), dtype=x.dtype)
        _, hs = jax.lax.scan(step, c0, (tm(i_g), tm(f_g), tm(o_g), tm(c_t)))
        h_out = jnp.moveaxis(hs, 0, 1).reshape(B, L, HIDDEN)
        return h_out @ W_out.T

    def _L0_ffn_ref(hidden_states, router_weight, router_bias, gate_up_proj, gate_up_proj_bias, down_proj, down_proj_bias):
        import jax, jax.numpy as jnp
        import numpy as np
        ALPHA = 1.702
        LIMIT = 7.0
        TOP_K = 4
        B, S, H = (1, 128, 256)
        E, D = (16, 256)
        batch, seq, hdim = hidden_states.shape
        x = hidden_states.reshape(-1, hdim)
        T = x.shape[0]
        logits = x @ router_weight.T + router_bias
        top_val, top_idx = jax.lax.top_k(logits, TOP_K)
        top_val = jax.nn.softmax(top_val, axis=-1)
        router_scores = jnp.zeros_like(logits).at[jnp.arange(T)[:, None], top_idx].set(top_val)
        gate_up = jnp.einsum('th,ehd->etd', x, gate_up_proj) + gate_up_proj_bias[:, None, :]
        gate = gate_up[..., ::2]
        up = gate_up[..., 1::2]
        gate = jnp.minimum(gate, LIMIT)
        up = jnp.clip(up, -LIMIT, LIMIT)
        glu = gate * jax.nn.sigmoid(gate * ALPHA)
        out = jnp.einsum('etd,edh->eth', (up + 1.0) * glu, down_proj) + down_proj_bias[:, None, :]
        out = out * router_scores.T[:, :, None]
        out = out.sum(axis=0)
        return out.reshape(batch, seq, hdim)
    x = L0_attn_x
    x = x + _layernorm(_L0_attn_ref(_layernorm(x, axis=-1), L0_attn_W_in, L0_attn_W_gate, L0_attn_b_gate, L0_attn_rms_w, L0_attn_W_out), axis=-1)
    x = x + _layernorm(_L0_ffn_ref(_layernorm(x, axis=-1), L0_ffn_router_weight, L0_ffn_router_bias, L0_ffn_gate_up_proj, L0_ffn_gate_up_proj_bias, L0_ffn_down_proj, L0_ffn_down_proj_bias), axis=-1)
    return x

_drawn_inputs = setup_inputs


def setup_inputs(seed=0):
    import zlib

    import numpy as np

    out = dict(_drawn_inputs(seed))
    spreads = {'L0_attn_b_gate': (0.0, 0.1), 'L0_attn_rms_w': (1.0, 0.2)}
    factors = {}
    for name, (base, spread) in spreads.items():
        noise = np.random.default_rng([zlib.crc32(name.encode()), seed]).standard_normal(out[name].shape)
        drawn = base * np.exp(spread * noise) if base else spread * noise
        out[name] = jnp.asarray(drawn.astype(out[name].dtype))
    for name, factor in factors.items():
        out[name] = (out[name] * factor).astype(out[name].dtype)
    return out
```

```python
import concourse.bass as bass
from concourse import mybir
from contextlib import ExitStack
import numpy as np

P = 128
BATCH, SEQ, DIM = 16, 256, 256
TOKENS = BATCH * SEQ
HEADS, HD = 4, 64
PAIRS = 2
KT = DIM // P
BLK = 512
BT = BLK // P
NBLK = TOKENS // BLK
NTILE = TOKENS // P
GATES = 4 * DIM
CHUNKS = GATES // P
E, TOPK, FF = 16, 4, 256
ROW = DIM + 2 * E
REGION = TOKENS + P
PAD0 = E * REGION
ZROWS = TOKENS * TOPK
TILES = -(-(ZROWS + E * (P - 1)) // P)
UN = 4
TURNS = -(-TILES // UN)
TILES = TURNS * UN
LIMIT, ALPHA = 7.0, 1.702
LN_EPS, RMS_EPS = 1e-5, 1e-6
MAGIC = float(0x5F3759DF)
PER_TURN = 96

C_IDENT, C_HALF, C_IOTA, C_BASE, C_DEST, C_SEL = 0, 128, 130, 146, 162, 178
C_TILE = C_SEL + 8 * P
C_TRI16 = C_TILE + TILES
C_PAD = C_TRI16 + E
C_DUMP = C_PAD + ROW
C_LEN = C_DUMP + UN
B_TRI, B_ONE, B_PICK = 0, 128, 256
B_LEN = B_PICK + E * P


def constants():
    c = np.zeros((P, C_LEN), np.float32)
    p = np.arange(P)
    c[:, C_IDENT:C_IDENT + P] = np.eye(P)
    c[:, C_HALF:C_HALF + 2] = (p[:, None] // HD) == np.arange(2)
    c[:, C_IOTA:C_IOTA + E] = np.arange(E)
    c[:, C_BASE:C_BASE + E] = np.arange(E) * REGION
    c[:, C_DEST:C_DEST + BT * TOPK] = (TOPK * (P * np.arange(BT)[None, :, None] + p[:, None, None])
                                       + np.arange(TOPK)).reshape(P, -1)
    for j in range(BT):
        for q in range(PAIRS):
            for half in range(2):
                lo = C_SEL + (j * PAIRS + q) * P + half * HD
                c[j * HEADS + 2 * q + half, lo:lo + HD] = 1.0
    c[:, C_TILE:C_TILE + TILES] = np.arange(TILES)
    c[:E, C_TRI16:C_TRI16 + E] = np.arange(E)[:, None] <= np.arange(E)
    c[:, C_PAD + DIM:C_PAD + DIM + E] = 2 * ZROWS
    c[:, C_DUMP:C_DUMP + UN] = ZROWS + P * np.arange(UN) + p[:, None]
    b = np.zeros((P, B_LEN), np.float32)
    b[:, B_TRI:B_TRI + P] = p[:, None] < p
    b[:, B_ONE:B_ONE + P] = 1.0
    for e in range(E):
        for part in range(3):
            b[32 * part + e, B_PICK + e * P:B_PICK + (e + 1) * P] = 1.0
    return c, b


class Link:

    def __init__(self, eng, sem):
        self.eng, self.sem, self.n, self.turn = eng, sem, 0, 0

    def __call__(self, ins, apart=False):
        ins.then_inc(self.sem, 1)
        self.n += 1
        self.eng.wait_ge(self.sem, self.n + self.turn)
        if apart:
            self.eng.nop(nofuse=True)

    def start(self, i, per):
        self.turn, self.per, self.first = i * per, per, self.n

    def stop(self, turns):
        assert self.n - self.first == self.per, (self.n - self.first, self.per)
        self.n, self.turn = self.first + self.per * turns, 0


def build(nc, x, w_in, w_gate, b_gate, rms_w, w_out, w_router, b_router, w_gu, b_gu, w_dn, b_dn,
          cst, cstb, out):
    f32, bf16 = mybir.dt.float32, mybir.dt.bfloat16
    i32, u32 = mybir.dt.int32, mybir.dt.uint32
    ALU = mybir.AluOpType
    ACT = mybir.ActivationFunctionType
    AX = mybir.AxisListType.X
    ds = bass.ds

    ctx = ExitStack()
    with ctx:
        def sb(name, shape, dt=f32):
            return ctx.enter_context(nc.sbuf_tensor(name, shape, dt))

        def sem(name):
            return ctx.enter_context(nc.semaphore(name))

        routed = nc.dram_tensor("routed", [PAD0 + P, ROW], f32, kind="Internal").ap()
        expert_out = nc.dram_tensor("expert_out", [ZROWS + UN * P, DIM], f32, kind="Internal").ap()

        X = sb("X", [P, NTILE, DIM])
        Wgu = sb("Wgu", [P, E * KT * 2 * FF])
        Wdn = sb("Wdn", [P, E * KT * DIM])
        K = sb("K", [P, C_LEN])
        KB = sb("KB", [P, B_LEN], bf16)
        Wd = sb("Wd", [P, NTILE, E])
        bias_src = sb("bias_src", [P, 2 * FF])
        bias_gu = sb("bias_gu", [P, 2 * FF], bf16)
        Bdn = sb("Bdn", [E, DIM])
        tab_row = sb("tab_row", [1, TILES], i32)
        tab_e = sb("tab_e", [1, TILES], i32)
        tab_pad = sb("tab_pad", [1, E], i32)
        small = sb("small", [P, 1024])
        arena = sb("arena", [P, 13200])
        PS = ctx.enter_context(nc.psum_tensor("PS", [P, 8, 512], f32))

        KBf = Wgu[:, 0:B_LEN]
        ident = K[:, C_IDENT:C_IDENT + P]
        triB, oneB = KB[:, B_TRI:B_TRI + P], KB[:, B_ONE:B_ONE + P]

        at = [0]

        def cut(n, parts=P):
            lo = at[0]
            at[0] += n
            assert at[0] <= 13200
            return arena[0:parts, lo:lo + n]

        WcT = cut(KT * GATES).rearrange("p (k g) -> p k g", k=KT)
        WoT = cut(PAIRS * DIM).rearrange("p (k g) -> p k g", k=PAIRS)
        WrT = cut(KT * E).rearrange("p (k g) -> p k g", k=KT)
        xn = cut(BT * DIM).rearrange("p (j d) -> p j d", j=BT)
        xT = cut(KT * BLK).rearrange("p (k t) -> p k t", k=KT)
        g_i = cut(PAIRS * BLK).rearrange("p (k t) -> p k t", k=PAIRS)
        g_c = cut(PAIRS * BLK).rearrange("p (k t) -> p k t", k=PAIRS)
        stage = at[0]
        g_o = [cut(PAIRS * BLK).rearrange("p (k t) -> p k t", k=PAIRS) for _ in range(2)]
        cell = [cut(PAIRS * BLK).rearrange("p (k t) -> p k t", k=PAIRS) for _ in range(2)]
        WgT = arena[:, stage:stage + KT * GATES].rearrange("p (k g) -> p k g", k=KT)
        WiT = arena[:, stage + KT * GATES:stage + KT * GATES + KT * DIM].rearrange("p (k g) -> p k g", k=KT)
        csq, g_f = [Wgu[:, 14 * 1024 + n * 1024:15 * 1024 + n * 1024].rearrange("p (k t) -> p k t", k=PAIRS)
                    for n in range(2)]
        late = E * KT * DIM // 2
        cn, hT, yn, x2T = [Wdn[:, late + n * 1024:late + (n + 1) * 1024].rearrange("p (k t) -> p k t", k=k)
                           for n, k in enumerate((PAIRS, PAIRS, BT, KT))]
        rows = [cut(BT * ROW).rearrange("p (j d) -> p j d", j=BT) for _ in range(2)]
        at[0] = 0
        xg = [cut(ROW) for _ in range(UN)]
        xgT = [cut(DIM).rearrange("p (k t) -> p k t", k=KT) for _ in range(2)]
        gate = [cut(FF) for _ in range(2)]
        up = [cut(FF) for _ in range(2)]
        sg = [cut(FF) for _ in range(2)]
        glu = [cut(FF) for _ in range(2)]
        act_ = [cut(FF) for _ in range(2)]
        actT = [cut(FF).rearrange("p (k t) -> p k t", k=KT) for _ in range(2)]
        yb = [cut(DIM) for _ in range(UN)]
        dst = [cut(1).bitcast(u32) for _ in range(UN)]
        dstf = [cut(1) for _ in range(UN)]
        wgt = [cut(1) for _ in range(UN)]
        at[0] = 0
        zin = [cut(TOPK * DIM).rearrange("p (k d) -> p k d", k=TOPK) for _ in range(4)]
        zs = [cut(2 * DIM).rearrange("p (k d) -> p k d", k=2) for _ in range(2)]
        sT = [cut(BT * P, E) for _ in range(2)]
        ws = [cut(BT * E).rearrange("p (j e) -> p j e", j=BT) for _ in range(2)]
        yz = [cut(BT * DIM).rearrange("p (j d) -> p j d", j=BT) for _ in range(2)]

        sat = [0]

        def tiny(n, dt=f32, parts=P):
            lo = sat[0]
            sat[0] += n
            assert sat[0] <= 1024
            v = small[0:parts, lo:lo + n]
            return v if dt == f32 else v.bitcast(dt)

        bG = tiny(CHUNKS)
        rmsw = tiny(1)
        bR = tiny(E)
        mv1 = tiny(NTILE * 2).rearrange("p (j s) -> p j s", s=2)
        r1 = tiny(NTILE)
        nv, na, nb_, ny = tiny(NTILE), tiny(NTILE), tiny(NTILE), tiny(NTILE)
        st2 = tiny(BT * 6).rearrange("p (j s) -> p j s", s=6)
        mv2 = tiny(BT * 2).rearrange("p (j s) -> p j s", s=2)
        mv3 = tiny(BT * 2).rearrange("p (j s) -> p j s", s=2)
        rs = tiny(BT + BT * HEADS)
        mr2, r3 = tiny(BT), tiny(BT)
        rT = tiny(P, parts=BT * HEADS)
        top = tiny(BT * 8).rearrange("p (j s) -> p j s", s=8)
        topi = tiny(BT * 8, u32).rearrange("p (j s) -> p j s", s=8)
        logit = tiny(BT * E).rearrange("p (j s) -> p j s", s=E)
        topf = tiny(BT * TOPK).rearrange("p (j s) -> p j s", s=TOPK)
        wexp = tiny(BT * TOPK).rearrange("p (j s) -> p j s", s=TOPK)
        wsum = tiny(BT)
        dest = tiny(BT * TOPK).rearrange("p (j s) -> p j s", s=TOPK)
        slotf = tiny(BT * TOPK).rearrange("p (j s) -> p j s", s=TOPK)
        slot = [tiny(BT * TOPK, i32) for _ in range(2)]
        cnt_col, nt_col, dl_col, end_col = [tiny(1, parts=E) for _ in range(4)]
        cnt_i = tiny(1, i32, parts=E)
        oh = sb("oh", [P, BT, TOPK, E])
        prod = sb("prod", [P, BT, TOPK, E])
        slot_e = sb("slot_e", [P, BT, E])
        chosen = sb("chosen", [P, BT, E], bf16)
        before = sb("before", [P, E], bf16)
        mstep = sb("mstep", [P, E])
        ended = sb("ended", [E, TILES])
        rowf = sb("rowf", [1, 2, TILES])

        s_const, s_w, s_moe = sem("s_const"), sem("s_w"), sem("s_moe")
        s_x = [sem(f"s_x{b}") for b in range(2)]
        bias_zero, bias_in, bias_done = sem("bias_zero"), sem("bias_in"), sem("bias_done")
        wc_mm, wc_copy, half_b, kb_ready = sem("wc_mm"), sem("wc_copy"), sem("half_b"), sem("kb_ready")
        xn_ready, xT_mm, xT_ready = sem("xn_ready"), sem("xT_mm"), sem("xT_ready")
        gate_mm, gate_act, f_ready = sem("gate_mm"), sem("gate_act"), sem("f_ready")
        cell_ready, csq_ready, ms_mm = sem("cell_ready"), sem("csq_ready"), sem("ms_mm")
        rms_ready, rT_mm, rT_ready, rb_mm = sem("rms_ready"), sem("rT_mm"), sem("rT_ready"), sem("rb_mm")
        cn_ready, tanh_ready, h_ready = sem("cn_ready"), sem("tanh_ready"), sem("h_ready")
        y_mm, r2_ready, yn_ready = sem("y_mm"), sem("r2_ready"), sem("yn_ready")
        x2_ready, x2T_mm, x2T_ready = sem("x2_ready"), sem("x2T_mm"), sem("x2T_ready")
        log_mm, wdiff, wexp_ready = sem("log_mm"), sem("wdiff"), sem("wexp_ready")
        chosen_ready, rank_mm, before_ready = sem("chosen_ready"), sem("rank_mm"), sem("before_ready")
        slot_ready = sem("slot_ready")
        rows_sent = [sem(f"rows_sent{b}") for b in range(2)]
        rows_free = sem("rows_free")
        v_link = sem("v_link")
        cnt_mm, nt_ready, end_mm, cmp_ready = sem("cnt_mm"), sem("nt_ready"), sem("end_mm"), sem("cmp_ready")
        tab_mm, tab_ready, pad_sent = sem("tab_mm"), sem("tab_ready"), sem("pad_sent")
        xg_in = [sem(f"xg_in{u}") for u in range(UN)]
        tr_mm, tr_ready, gu_mm = sem("tr_mm"), sem("tr_ready"), sem("gu_mm")
        gate_ready, sg_ready, act_ready = sem("gate_ready"), sem("sg_ready"), sem("act_ready")
        aT_mm, aT_ready, y2_mm = sem("aT_mm"), sem("aT_ready"), sem("y2_mm")
        y2_ready = sem("y2_ready")
        dst_copied, dst_ready = sem("dst_copied"), sem("dst_ready")
        y_sent = [sem(f"y_sent{u}") for u in range(UN)]
        z_in = [sem(f"z_in{u}") for u in range(4)]
        zs_ready, zs_free = sem("zs_ready"), sem("zs_free")
        sT_mm, sT_ready = sem("sT_mm"), sem("sT_ready")
        rz_ready, yz_ready, yo_ready = sem("rz_ready"), sem("yz_ready"), sem("yo_ready")
        out_sent, ws_ready = sem("out_sent"), sem("ws_ready")

        block = ctx.enter_context(nc.Block())
        x_v = x.rearrange("(n p) d -> p n d", p=P)
        out_v = out.rearrange("(n p) d -> p n d", p=P)

        def steps(eng, step, link=None, per=0):
            step(0, 0), step(1, 1)
            turns = (NBLK - 3) // 2
            with eng.Fori(0, turns) as i:
                if link:
                    link.start(i, per)
                step(2 * i + 2, 2, i)
                step(2 * i + 3, 3, i)
            if link:
                link.stop(turns)
            for s in range(2 + 2 * turns, NBLK + 2):
                step(s, s)

        def tiles(eng, step):
            for j in range(UN + 2):
                step(j, j)
            with eng.Fori(0, TURNS - 2) as i:
                for u in range(UN):
                    step(UN * i + (UN + 2 + u), UN + 2 + u, i)
            for j in range(TILES - 2, TILES + 2):
                step(j, j)

        def on(s0, lag):
            return 0 <= s0 - lag < NBLK

        @block.sync
        def _(sp):
            sp.sem_inc(rows_free, 2)
            sp.sem_inc(zs_free, 2)
            sp.sem_inc(y2_ready, 2)
            sp.sem_inc(yz_ready, 2)
            sp.dma_start(K[:, :], cst).then_inc(s_const, 16)
            sp.dma_start(KBf, cstb).then_inc(s_const, 16)
            for src, dstt in ((w_in, WiT), (w_gate, WgT), (w_out, WoT), (w_router, WrT)):
                sp.dma_start(dstt, src).then_inc(s_w, 16)
            sp.dma_start(bG, b_gate).then_inc(s_w, 16)
            sp.dma_start(rmsw, rms_w).then_inc(s_w, 16)
            sp.dma_start(bR, b_router).then_inc(s_w, 16)
            for b in range(NBLK):
                if b >= 2:
                    sp.wait_ge(s_x[b % 2], 16 * (b // 2))
                sp.dma_start(X[:, BT * b:BT * (b + 1), :], x_v[:, BT * b:BT * (b + 1), :]).then_inc(s_x[b % 2], 16)
            sp.dma_start(Bdn[:, :], b_dn).then_inc(s_moe, 16)
            sp.wait_ge(kb_ready, 1)
            q = E * KT * 2 * FF // 8
            for n in range(7):
                sp.dma_start(Wgu[:, n * q:(n + 1) * q], w_gu[:, n * q:(n + 1) * q]).then_inc(s_moe, 16)
            q = E * KT * DIM // 4
            for n in range(2):
                sp.dma_start(Wdn[:, n * q:(n + 1) * q], w_dn[:, n * q:(n + 1) * q]).then_inc(s_moe, 16)
            sp.wait_ge(bias_zero, 1)
            for part in range(3):
                sp.dma_start(bias_src[32 * part:32 * part + E, :], b_gu).then_inc(bias_in, 16)
            sp.wait_ge(before_ready, NBLK + 1)
            sp.dma_start(Wgu[:, 14 * 1024:], w_gu[:, 14 * 1024:]).then_inc(s_moe, 16)
            for n in range(2, 4):
                sp.dma_start(Wdn[:, n * q:(n + 1) * q], w_dn[:, n * q:(n + 1) * q]).then_inc(s_moe, 16)

            sp.wait_ge(tab_ready, 1)
            pad = K[:, C_PAD:C_PAD + ROW]
            for e in range(E):
                first = sp.value_load(tab_pad[0:1, e:e + 1], min_val=e * REGION, max_val=e * REGION + TOKENS)
                sp.dma_start(routed[ds(first, P), :], pad).then_inc(pad_sent, 16)
            sp.dma_start(routed[PAD0:PAD0 + P, :], pad).then_inc(pad_sent, 16)
            sp.wait_ge(pad_sent, 16 * (E + 1))
            for b in range(2):
                sp.wait_ge(rows_sent[b], 16 * BT * TOPK * NBLK // 2)

            def load_tile(j, u):
                r = sp.value_load(tab_row[0:1, ds(j, 1)], min_val=0, max_val=PAD0)
                sp.dma_start(xg[u], routed[ds(r, P), :]).then_inc(xg_in[u], 16)

            for u in range(UN):
                load_tile(u, u)
            with sp.Fori(1, TURNS) as i:
                for u in range(UN):
                    sp.wait_ge(tr_mm, UN * i + (u + 1 - UN))
                    sp.wait_ge(dst_ready, UN * i + (u + 1 - UN))
                    load_tile(UN * i + u, u)

            for u in range(UN):
                sp.wait_ge(y_sent[u], 16 * TURNS)
            z_v = expert_out[0:ZROWS, :].rearrange("(n p k) d -> n p k d", p=P, k=TOPK)

            def load_z(n, u):
                sp.dma_start(zin[u], z_v[ds(n, 1), :, :, :].rearrange("n p k d -> (n p) k d")).then_inc(z_in[u], 16)

            for u in range(4):
                load_z(u, u)
            with sp.Fori(1, NTILE // 4) as i:
                for u in range(4):
                    sp.wait_ge(zs_ready, 4 * i + (u + 1 - 4))
                    load_z(4 * i + u, u)
            sp.wait_ge(out_sent, 16 * NBLK)

        @block.tensor
        def _(pe):
            mm = nc.tensor.matmul

            pe.wait_ge(s_w, 16 * 7)
            for n in range(2):
                for m in range(KT):
                    for k in range(KT):
                        last = mm(PS[:, 2 * n + m, :], WiT[:, k, m * P:(m + 1) * P],
                                  WgT[:, k, n * 512:(n + 1) * 512], start=(k == 0), stop=(k == KT - 1))
                    last.then_inc(wc_mm, 1)

            def transposes_x(t):
                pe.wait_ge(xn_ready, t + 1)
                for k in range(KT):
                    for j in range(BT):
                        last = nc.tensor.transpose(PS[:, k, j * P:(j + 1) * P], xn[:, j, k * P:(k + 1) * P], ident)
                    last.then_inc(xT_mm, 1)

            def gates(t, c, first):
                if c == 0:
                    pe.wait_ge(xT_ready, 2 * t + 2)
                if first or c >= 2:
                    pe.wait_ge(gate_act, 8 * t + (c - 1))
                for k in range(KT):
                    last = mm(PS[:, 2 + c % 2, :], WcT[:, k, c * P:(c + 1) * P], xT[:, k, :],
                              start=(k == 0), stop=(k == KT - 1))
                last.then_inc(gate_mm, 1)

            def mean_square(t):
                pe.wait_ge(csq_ready, t + 1)
                for j in range(BT):
                    for q in range(PAIRS):
                        last = mm(PS[:, 6, HEADS * j + 2 * q:HEADS * j + 2 * q + 2], csq[:, q, j * P:(j + 1) * P],
                                  K[:, C_HALF:C_HALF + 2], start=True, stop=True)
                last.then_inc(ms_mm, 1)

            def rms_transpose(t):
                pe.wait_ge(rms_ready, t + 1)
                nc.tensor.transpose(PS[0:BT * HEADS, 6, P:2 * P], rs[:, BT:BT + BT * HEADS], ident).then_inc(rT_mm, 1)

            def rms_spread(t, later):
                pe.wait_ge(rT_ready, t + 1)
                if later:
                    pe.wait_ge(yn_ready, t)
                for q in range(PAIRS):
                    for j in range(BT):
                        lo = C_SEL + (j * PAIRS + q) * P
                        last = mm(PS[:, 4 + q, j * P:(j + 1) * P], K[0:BT * HEADS, lo:lo + P], rT,
                                  start=True, stop=True)
                last.then_inc(rb_mm, 1)

            def out_product(t):
                pe.wait_ge(h_ready, t + 1)
                for j in range(BT):
                    for q in range(PAIRS):
                        last = mm(PS[:, 4 + j // 2, (j % 2) * DIM:(j % 2 + 1) * DIM], hT[:, q, j * P:(j + 1) * P],
                                  WoT[:, q, :], start=(q == 0), stop=(q == PAIRS - 1))
                last.then_inc(y_mm, 1)

            def transposes_x2(t, rw):
                pe.wait_ge(x2_ready, t + 1)
                for k in range(KT):
                    for j in range(BT):
                        last = nc.tensor.transpose(PS[:, k, j * P:(j + 1) * P], rw[:, j, k * P:(k + 1) * P], ident)
                    last.then_inc(x2T_mm, 1)

            def logits(t):
                pe.wait_ge(x2T_ready, 2 * t + 2)
                for j in range(BT):
                    for k in range(KT):
                        last = mm(PS[:, 7, E * j:E * (j + 1)], x2T[:, k, j * P:(j + 1) * P], WrT[:, k, :],
                                  start=(k == 0), stop=(k == KT - 1))
                last.then_inc(log_mm, 1)

            def ranks(t):
                pe.wait_ge(chosen_ready, t + 1)
                pe.wait_ge(before_ready, t + 1)
                R = PS[:, 7, 256:256 + BT * E].rearrange("p (j e) -> p j e", e=E)
                mm(R, triB, chosen[:, :, :], start=True, stop=False)
                mm(R, oneB, before[:, :].unsqueeze(1).to_broadcast([P, BT, E]), start=False, stop=False)
                for j in range(BT - 1):
                    last = mm(R[:, j + 1:BT, :], oneB,
                              chosen[:, j:j + 1, :].to_broadcast([P, BT - 1 - j, E]),
                              start=False, stop=(j == BT - 2))
                last.then_inc(rank_mm, 1)

            def step(s, s0, i=None):
                new, mid, old = on(s0, 0), on(s0, 1), on(s0, 2)
                for c in range(CHUNKS):
                    if new:
                        gates(s, c, s0 > 0)
                    if c == 2 and mid:
                        mean_square(s - 1)
                    if c == 4 and mid:
                        rms_transpose(s - 1)
                    if c == 5 and mid:
                        rms_spread(s - 1, s0 > 1)
                    if c == 6 and old:
                        transposes_x2(s - 2, rows[s0 % 2])
                if old:
                    logits(s - 2)
                if mid:
                    out_product(s - 1)
                if on(s0, -1):
                    transposes_x(s + 1)
                if old:
                    ranks(s - 2)

            pe.wait_ge(s_const, 32)
            pe.wait_ge(wc_copy, 4)
            transposes_x(0)
            pe.wait_ge(kb_ready, 1)
            steps(pe, step)

            pe.wait_ge(before_ready, NBLK + 1)
            mm(PS[0:1, 0, 0:E], KB[:, B_ONE:B_ONE + 1], before[:, :], start=True, stop=True)
            mm(PS[0:E, 1, 0:1], before[:, :], KB[:, B_ONE:B_ONE + 1], start=True, stop=True).then_inc(cnt_mm, 1)
            pe.wait_ge(nt_ready, 1)
            mm(PS[0:E, 2, 0:1], K[0:E, C_TRI16:C_TRI16 + E], nt_col, start=True, stop=True).then_inc(end_mm, 1)
            pe.wait_ge(cmp_ready, 1)
            mm(PS[0:1, 3, 0:TILES], K[0:E, C_TRI16 + E - 1:C_TRI16 + E], ended[:, :], start=True, stop=True)
            mm(PS[0:1, 4, 0:TILES], dl_col, ended[:, :], start=True, stop=True).then_inc(tab_mm, 1)

            pe.wait_ge(s_moe, 16 * 13)
            pe.wait_ge(bias_done, 1)
            pe.wait_ge(tab_ready, 1)

            def tile_transposes(j, uj, i):
                pe.wait_ge(xg_in[uj % UN], 16 * (uj // UN + 1) if i is None else 16 * i + 16 * (uj // UN + 1))
                for k in range(KT):
                    last = nc.tensor.transpose(PS[:, uj % 2, k * P:(k + 1) * P],
                                               xg[uj % UN][:, k * P:(k + 1) * P], ident)
                last.then_inc(tr_mm, 1)

            def gate_up(j, uj):
                e = pe.value_load(tab_e[0:1, ds(j, 1)], min_val=0, max_val=E - 1)
                acc = PS[:, 2 + uj % 2, :]
                mm(acc, KB[:, ds(e * P + B_PICK, P)], bias_gu[:, :], start=True, stop=False)
                pe.wait_ge(tr_ready, j + 1)
                for k in range(KT):
                    last = mm(acc, xgT[uj % 2][:, k, :], Wgu[:, ds(e * (KT * 2 * FF) + k * 2 * FF, 2 * FF)],
                              start=False, stop=(k == KT - 1))
                last.then_inc(gu_mm, 1)

            def act_transposes(j, uj):
                pe.wait_ge(act_ready, j + 1)
                for k in range(KT):
                    last = nc.tensor.transpose(PS[:, 4 + uj % 2, k * P:(k + 1) * P],
                                               act_[uj % 2][:, k * P:(k + 1) * P], ident)
                last.then_inc(aT_mm, 1)

            def down(j, uj):
                e = pe.value_load(tab_e[0:1, ds(j, 1)], min_val=0, max_val=E - 1)
                pe.wait_ge(y2_ready, j + 1)
                pe.wait_ge(aT_ready, j + 1)
                for k in range(KT):
                    last = mm(PS[:, 6 + uj % 2, 0:DIM], actT[uj % 2][:, k, :],
                              Wdn[:, ds(e * (KT * DIM) + k * DIM, DIM)], start=(k == 0), stop=(k == KT - 1))
                last.then_inc(y2_mm, 1)

            def tile_step(j, uj, i=None):
                if uj < 2:
                    if uj == 0:
                        tile_transposes(0, 0, None)
                    tile_transposes(j + 1, uj + 1, None)
                    gate_up(j, uj)
                    return
                act_transposes(j - 2, uj - 2)
                if i is not None or j + 1 < TILES:
                    tile_transposes(j + 1, uj + 1, i)
                if i is not None or j < TILES:
                    gate_up(j, uj)
                down(j - 2, uj - 2)

            tiles(pe, tile_step)

            def combine(g, b):
                pe.wait_ge(ws_ready, g + 1)
                for u in range(BT):
                    last = nc.tensor.transpose(PS[0:E, b, u * P:(u + 1) * P], ws[b][:, u, :], ident)
                last.then_inc(sT_mm, 1)
                pe.wait_ge(sT_ready, g + 1)
                pe.wait_ge(yz_ready, g + 1)
                for u in range(BT):
                    acc = PS[:, 2 + 2 * b + u // 2, (u % 2) * DIM:(u % 2 + 1) * DIM]
                    mm(acc, sT[b][:, u * P:(u + 1) * P], Bdn[:, :], start=True, stop=False)
                    pe.wait_ge(zs_ready, BT * g + (u + 1))
                    mm(acc, ident, zs[u % 2][:, 0, :], start=False, stop=False)
                    mm(acc, ident, zs[u % 2][:, 1, :], start=False, stop=True).then_inc(zs_free, 1)

            with pe.Fori(0, NBLK // 2) as i:
                for b in range(2):
                    combine(2 * i + b, b)

        @block.scalar
        def _(act):
            def copy(o, i, **kw):
                return nc.scalar.activation(o, i, ACT.Copy, **kw)

            for n in range(2):
                for m in range(KT):
                    act.wait_ge(wc_mm, 2 * n + m + 1)
                    copy(WcT[:, m, n * 512:(n + 1) * 512], PS[:, 2 * n + m, :]).then_inc(wc_copy, 1)

            def evac_x(t):
                for k in range(KT):
                    act.wait_ge(xT_mm, 2 * t + (k + 1))
                    copy(xT[:, k, :], PS[:, k, :]).then_inc(xT_ready, 1)

            def gate_chunk(t, c, s0):
                kind, q = c // 2, c % 2
                if c == 0 and s0 >= 1:
                    act.wait_ge(cell_ready, t)
                if c == 6 and s0 >= 2:
                    act.wait_ge(h_ready, t - 1)
                act.wait_ge(gate_mm, 8 * t + (c + 1))
                nc.scalar.activation((g_c, g_i, g_f, g_o[s0 % 2])[kind][:, q, :], PS[:, 2 + c % 2, :],
                                     ACT.Exp if kind == 1 else ACT.Tanh, bias=bG[:, c:c + 1],
                                     scale=1.0 if kind < 2 else 0.5).then_inc(gate_act, 1)
                if c == 5:
                    act.wait_ge(gate_act, 8 * t + 6)
                    copy(g_f, g_f, bias=0.5, scale=0.5).then_inc(f_ready, 1)

            def square(t, par, later):
                act.wait_ge(cell_ready, t + 1)
                if later:
                    act.wait_ge(ms_mm, t)
                nc.scalar.activation(csq, cell[par], ACT.Square).then_inc(csq_ready, 1)

            def rms_row(t):
                act.wait_ge(rT_mm, t + 1)
                copy(rT, PS[0:BT * HEADS, 6, P:2 * P]).then_inc(rT_ready, 1)

            def tanh_c(t):
                act.wait_ge(cn_ready, t + 1)
                nc.scalar.activation(cn, cn, ACT.Tanh, scale=rmsw).then_inc(tanh_ready, 1)

            def norm_y(t):
                act.wait_ge(r2_ready, t + 1)
                for j in range(BT):
                    last = nc.scalar.activation(yn[:, j, :], PS[:, 4 + j // 2, (j % 2) * DIM:(j % 2 + 1) * DIM],
                                                ACT.Identity, bias=mr2[:, j:j + 1], scale=rs[:, j:j + 1])
                last.then_inc(yn_ready, 1)

            def evac_x2(t):
                for k in range(KT):
                    act.wait_ge(x2T_mm, 2 * t + (k + 1))
                    copy(x2T[:, k, :], PS[:, k, :]).then_inc(x2T_ready, 1)

            def weights_exp(t):
                act.wait_ge(wdiff, t + 1)
                nc.scalar.activation(wexp, wexp, ACT.Exp).then_inc(wexp_ready, 1)

            def step(s, s0, i=None):
                new, mid, old = on(s0, 0), on(s0, 1), on(s0, 2)
                for c in range(CHUNKS):
                    if c == 2 and mid:
                        square(s - 1, (s0 - 1) % 2, s0 > 1)
                    if new:
                        gate_chunk(s, c, s0)
                    if c == 3 and old:
                        norm_y(s - 2)
                    if c == 4 and mid:
                        rms_row(s - 1)
                    if c == 5 and mid:
                        tanh_c(s - 1)
                    if c == 6 and old:
                        evac_x2(s - 2)
                if on(s0, -1):
                    evac_x(s + 1)
                if old:
                    weights_exp(s - 2)

            act.wait_ge(half_b, 1)
            evac_x(0)
            steps(act, step)

            def evac_tile(j, uj):
                act.wait_ge(tr_mm, j + 1)
                copy(xgT[uj % 2], PS[:, uj % 2, 0:DIM].rearrange("p (k t) -> p k t", k=KT)).then_inc(tr_ready, 1)

            def tile_step(j, uj, i=None):
                running = i is not None
                if uj == 0:
                    evac_tile(0, 0)
                if uj >= 2:
                    act.wait_ge(aT_mm, j - 1)
                    copy(actT[uj % 2], PS[:, 4 + uj % 2, 0:FF].rearrange("p (k t) -> p k t", k=KT)).then_inc(aT_ready, 1)
                if running or j + 1 < TILES:
                    evac_tile(j + 1, uj + 1)
                if running or j < TILES:
                    act.wait_ge(gate_ready, j + 1)
                    nc.scalar.activation(sg[uj % 2], gate[uj % 2], ACT.Tanh, scale=ALPHA / 2).then_inc(sg_ready, 1)
                if uj >= 2:
                    u = (uj - 2) % UN
                    act.wait_ge(dst_ready, j - 1)
                    if uj - 2 >= UN:
                        turn = (uj - 2) // UN
                        act.wait_ge(y_sent[u], 16 * i + 16 * turn if running else 16 * turn)
                    act.wait_ge(y2_mm, j - 1)
                    copy(yb[u], PS[:, 6 + uj % 2, 0:DIM], scale=wgt[u]).then_inc(y2_ready, 1)

            tiles(act, tile_step)

            for u in range(UN):
                act.wait_ge(y_sent[u], 16 * TURNS)

            def store(g):
                act.wait_ge(yo_ready, g + 1)
                act.dma_start(out_v[:, ds(BT * g, BT), :], X[:, ds(BT * g, BT), :]).then_inc(out_sent, 16)

            def stage_weights(g, b):
                copy(ws[b], Wd[:, ds(BT * g, BT), :]).then_inc(ws_ready, 1)

            def group(g, b, later, more=True):
                act.wait_ge(sT_mm, g + 1)
                if more:
                    stage_weights(g + 1, 1 - b)
                copy(sT[b], PS[0:E, b, :]).then_inc(sT_ready, 1)
                act.wait_ge(rz_ready, g + 1)
                for u in range(BT):
                    last = nc.scalar.activation(yz[b][:, u, :], PS[:, 2 + 2 * b + u // 2, (u % 2) * DIM:(u % 2 + 1) * DIM],
                                                ACT.Identity, bias=mr2[:, u:u + 1], scale=rs[:, u:u + 1])
                last.then_inc(yz_ready, 1)
                if later:
                    store(g - 1)

            stage_weights(0, 0)
            group(0, 0, False)
            with act.Fori(0, NBLK // 2 - 1) as i:
                group(2 * i + 1, 1, True)
                group(2 * i + 2, 0, True)
            group(NBLK - 1, 1, True, False)
            store(NBLK - 1)

        @block.gpsimd
        def _(pool):
            def wait(s, n):
                pool.wait_ge(s, n)
                if not isinstance(n, int):
                    pool.nop(nofuse=True)

            def step(s, s0, i=None):
                if on(s0, 2):
                    wait(slot_ready, s - 1)
                    for jk in range(BT * TOPK):
                        idx = slot[s0 % 2][:, jk:jk + 1].bitcast(u32)
                        pool.indirect_dma_start(routed, bass.IndirectOffsetOnAxis(ap=idx, axis=0),
                                                rows[s0 % 2][:, jk // TOPK, :], None).then_inc(rows_sent[s0 % 2], 16)
                    n = 16 * BT * TOPK
                    pool.wait_ge(rows_sent[s0 % 2], n * (s0 // 2) if i is None else n * i + n * (s0 // 2))
                    pool.sem_inc(rows_free, 1)

            steps(pool, step)

            pool.wait_ge(tab_ready, 1)

            def tile_step(j, uj, i=None):
                running = i is not None
                if uj >= 2:
                    u = (uj - 2) % UN
                    wait(y2_ready, j + 1)
                    pool.indirect_dma_start(expert_out, bass.IndirectOffsetOnAxis(ap=dst[u], axis=0),
                                            yb[u], None).then_inc(y_sent[u], 16)
                if running or j < TILES:
                    u = uj % UN
                    e = pool.value_load(tab_e[0:1, ds(j, 1)], min_val=0, max_val=E - 1)
                    turn = uj // UN
                    if turn:
                        wait(y_sent[u], 16 * i + 16 * turn if running else 16 * turn)
                    wait(xg_in[u], 16 * i + (16 + 16 * turn) if running else 16 + 16 * turn)
                    pool.tensor_copy(wgt[u], xg[u][:, ds(e + (DIM + E), 1)])
                    pool.tensor_copy(dstf[u], xg[u][:, ds(e + DIM, 1)]).then_inc(dst_copied, 1)
                    wait(dst_copied, j + 1)
                    pool.tensor_scalar(dst[u], dstf[u], K[:, C_DUMP + u:C_DUMP + u + 1], None,
                                       ALU.min).then_inc(dst_ready, 1)

            tiles(pool, tile_step)

            def pair_sums(n, u, i):
                wait(z_in[u], 16 * i + 16)
                wait(zs_free, n + 1)
                pool.tensor_tensor(zs[u % 2], zin[u][:, 0:2, :], zin[u][:, 2:4, :], ALU.add).then_inc(zs_ready, 1)

            with pool.Fori(0, NTILE // 4) as i:
                for u in range(4):
                    pair_sums(4 * i + u, u, i)

        @block.vector
        def _(dve):
            v = nc.vector
            L = Link(dve, v_link)

            def newton(w, o, last=None):
                a, b, y, s = na[:, 0:w], nb_[:, 0:w], ny[:, 0:w], nv[:, 0:w]
                L(v.tensor_scalar(a.bitcast(i32), s.bitcast(i32), 1, None, ALU.logical_shift_right))
                L(v.tensor_scalar(y.bitcast(i32), a.bitcast(i32), -1.0, MAGIC, ALU.mult, ALU.add))
                for n in range(3):
                    L(v.tensor_tensor(a, y, y, ALU.mult))
                    L(v.scalar_tensor_tensor(b, a, -0.5, s, ALU.mult, ALU.mult))
                    (last if last and n == 2 else L)(
                        v.scalar_tensor_tensor(y if n < 2 else o, b, 1.5, y, ALU.add, ALU.mult))

            v.memset(bias_src[:, :], 0.0).then_inc(bias_zero, 1)
            v.memset(before[:, :], 0.0).then_inc(before_ready, 1)
            dve.wait_ge(s_w, 16 * 7)
            v.tensor_scalar(bG[:, 4:8], bG[:, 4:8], 0.5, None, ALU.mult).then_inc(half_b, 1)
            dve.wait_ge(s_const, 32)
            v.tensor_copy(KB[:, :], KBf).then_inc(kb_ready, 1)
            L(v.tensor_copy(dest, K[:, C_DEST:C_DEST + BT * TOPK].rearrange("p (j k) -> p j k", k=TOPK)))

            with dve.Fori(0, NBLK // 2) as i:
                L.start(i, 6)
                for b in range(2):
                    dve.wait_ge(s_x[b], 16 * i + 16)
                    dve.nop(nofuse=True)
                    for j in range(BT):
                        last = v.bn_stats(st2[:, j, :], X[:, ds(2 * BT * i + (BT * b + j), 1), :].rearrange("p n d -> p (n d)"))
                    L(last, True)
                    for j in range(BT):
                        last = v.bn_aggr(mv2[:, j, :], st2[:, j, :])
                    L(last)
                    L(v.tensor_copy(mv1[:, ds(2 * BT * i + BT * b, BT), :], mv2))
            L.stop(NBLK // 2)
            L(v.tensor_scalar(nv, mv1[:, :, 1], LN_EPS, None, ALU.add))
            newton(NTILE, r1)

            def norm_x(t, later):
                if later:
                    dve.wait_ge(xT_mm, 2 * t)
                for j in range(BT):
                    n = ds(BT * t + j, 1)
                    last = v.tensor_scalar(xn[:, j, :], X[:, n, :].rearrange("p n d -> p (n d)"),
                                           mv1[:, n, 0], r1[:, n], ALU.subtract, ALU.mult)
                last.then_inc(xn_ready, 1)

            def scan(t, par):
                dve.wait_ge(gate_act, 8 * t + 4)
                L(v.tensor_tensor(g_i, g_i, g_c, ALU.mult))
                dve.wait_ge(f_ready, t + 1)
                for q in range(PAIRS):
                    for b in range(BLK // SEQ):
                        w = slice(b * SEQ, (b + 1) * SEQ)
                        last = v.tensor_tensor_scan(cell[par][:, q, w], g_f[:, q, w], g_i[:, q, w], 0.0,
                                                    ALU.mult, ALU.add)
                last.then_inc(cell_ready, 1)

            def stats(src, mv, eps):
                dve.nop(nofuse=True)
                for j in range(BT):
                    last = v.bn_stats(st2[:, j, :], src(j))
                L(last, True)
                for j in range(BT):
                    last = v.bn_aggr(mv[:, j, :], st2[:, j, :])
                L(last)
                L(v.tensor_scalar(nv[:, 0:BT], mv[:, :, 1], eps, None, ALU.add))

            def block_norms(t_y, t_c, mid, old):
                lo = 0 if old else BT
                if old:
                    dve.wait_ge(y_mm, t_y + 1)
                    stats(lambda j: PS[:, 4 + j // 2, (j % 2) * DIM:(j % 2 + 1) * DIM], mv2, 4 * LN_EPS)
                elif mid:
                    L(v.memset(nv[:, 0:BT], 1.0))
                if mid:
                    dve.wait_ge(ms_mm, t_c + 1)
                    L(v.tensor_scalar(nv[:, BT:BT + BT * HEADS], PS[:, 6, 0:BT * HEADS], 1.0 / HD, RMS_EPS,
                                      ALU.mult, ALU.add))

                    def done(ins):
                        ins.then_inc(rms_ready, 1)
                        dve.wait_ge(rms_ready, t_c + 1)
                    newton(BT + BT * HEADS, rs, done)
                else:
                    newton(BT, rs[:, 0:BT])
                if old:
                    v.scalar_tensor_tensor(mr2, mv2[:, :, 0], -1.0, rs[:, 0:BT], ALU.mult, ALU.mult).then_inc(r2_ready, 1)

            def scale_cell(t, par):
                dve.wait_ge(rb_mm, t + 1)
                v.tensor_tensor(cn, cell[par], PS[:, 4:6, :], ALU.mult).then_inc(cn_ready, 1)

            def hidden(t, par):
                dve.wait_ge(tanh_ready, t + 1)
                v.scalar_tensor_tensor(hT, g_o[par], 1.0, cn, ALU.add, ALU.mult).then_inc(h_ready, 1)

            def residual(t, par):
                Xb = X[:, ds(BT * t, BT), :]
                dve.wait_ge(yn_ready, t + 1)
                L(v.tensor_tensor(Xb, Xb, yn, ALU.add))
                stats(lambda j: X[:, ds(BT * t + j, 1), :].rearrange("p n d -> p (n d)"), mv3, LN_EPS)
                newton(BT, r3)
                dve.wait_ge(rows_free, t + 1)
                for j in range(BT):
                    last = v.tensor_scalar(rows[par][:, j, 0:DIM], X[:, ds(BT * t + j, 1), :].rearrange("p n d -> p (n d)"),
                                           mv3[:, j, 0:1], r3[:, j:j + 1], ALU.subtract, ALU.mult)
                last.then_inc(x2_ready, 1)

            JK = [P, BT, TOPK, E]

            def choose(t, par):
                dve.wait_ge(log_mm, t + 1)
                L(v.tensor_tensor(logit, PS[:, 7, 0:BT * E].rearrange("p (j e) -> p j e", e=E),
                                  bR.unsqueeze(1).to_broadcast([P, BT, E]), ALU.add), True)
                for j in range(BT):
                    last = v.max(top[:, j, :], logit[:, j, :])
                L(last, True)
                for j in range(BT):
                    last = v.max_index(topi[:, j, :], top[:, j, :], logit[:, j, :])
                L(last)
                v.tensor_tensor(wexp, top[:, :, 0:TOPK], top[:, :, 0:1].to_broadcast([P, BT, TOPK]),
                                ALU.subtract).then_inc(wdiff, 1)
                L(v.tensor_copy(topf, topi[:, :, 0:TOPK]))
                L(v.tensor_tensor(oh[:, :, :, :], K[:, C_IOTA:C_IOTA + E].unsqueeze(1).unsqueeze(1).to_broadcast(JK),
                                  topf.unsqueeze(3).to_broadcast(JK), ALU.is_equal))
                with nc.allow_low_precision("counts up to four are exact in bfloat16"):
                    v.tensor_reduce(chosen[:, :, :], oh[:, :, :, :].rearrange("p j k e -> p j e k"), AX,
                                    ALU.add).then_inc(chosen_ready, 1)

            def spread(src, o):
                L(v.tensor_tensor(prod[:, :, :, :], oh[:, :, :, :], src.unsqueeze(3).to_broadcast(JK), ALU.mult))
                L(v.tensor_reduce(o, prod[:, :, :, :].rearrange("p j k e -> p j e k"), AX, ALU.add))

            def row_tails(t, par):
                spread(dest, rows[par][:, :, DIM:DIM + E])
                L(v.tensor_scalar(dest, dest, float(TOPK * BLK), None, ALU.add))
                dve.wait_ge(wexp_ready, t + 1)
                L(v.tensor_reduce(wsum, wexp, AX, ALU.add))
                L(v.reciprocal(wsum, wsum))
                L(v.tensor_tensor(wexp, wexp, wsum.unsqueeze(2).to_broadcast([P, BT, TOPK]), ALU.mult))
                Wb = Wd[:, ds(BT * t, BT), :]
                spread(wexp, Wb)
                L(v.tensor_scalar(rows[par][:, :, DIM + E:ROW], Wb, 0.5, None, ALU.mult))

            def slots(t, par):
                dve.wait_ge(rank_mm, t + 1)
                L(v.tensor_tensor(slot_e[:, :, :], PS[:, 7, 256:256 + BT * E].rearrange("p (j e) -> p j e", e=E),
                                  K[:, C_BASE:C_BASE + E].unsqueeze(1).to_broadcast([P, BT, E]), ALU.add))
                L(v.tensor_tensor(prod[:, :, :, :], oh[:, :, :, :],
                                  slot_e[:, :, :].unsqueeze(2).to_broadcast(JK), ALU.mult))
                L(v.tensor_reduce(slotf, prod[:, :, :, :], AX, ALU.add))
                v.tensor_copy(slot[par].rearrange("p (j k) -> p j k", k=TOPK), slotf).then_inc(slot_ready, 1)
                L(v.tensor_reduce(mstep[:, :], chosen[:, :, :].rearrange("p j e -> p e j"), AX, ALU.add))
                v.tensor_tensor(before[:, :], before[:, :], mstep[:, :], ALU.add).then_inc(before_ready, 1)

            def step(s, s0, i=None):
                new, mid, old = on(s0, 0), on(s0, 1), on(s0, 2)
                pm, po = (s0 - 1) % 2, s0 % 2
                if mid:
                    scan(s - 1, pm)
                block_norms(s - 2, s - 1, mid, old) if mid or old else None
                if mid:
                    scale_cell(s - 1, pm)
                if old:
                    residual(s - 2, po)
                if mid:
                    hidden(s - 1, pm)
                if on(s0, -1):
                    norm_x(s + 1, True)
                if old:
                    choose(s - 2, po)
                    row_tails(s - 2, po)
                    slots(s - 2, po)

            norm_x(0, False)
            steps(dve, step, L, PER_TURN)

            dve.wait_ge(cnt_mm, 1)
            L(v.tensor_tensor(tab_pad[:, :], PS[0:1, 0, 0:E], K[0:1, C_BASE:C_BASE + E], ALU.add))
            L(v.tensor_scalar(cnt_i, PS[0:E, 1, 0:1], float(P - 1), None, ALU.add))
            L(v.tensor_scalar(cnt_i, cnt_i, 7, None, ALU.logical_shift_right))
            L(v.tensor_copy(nt_col, cnt_i))
            v.tensor_scalar(dl_col, nt_col, -float(P), float(REGION), ALU.mult, ALU.add).then_inc(nt_ready, 1)
            dve.wait_ge(end_mm, 1)
            L(v.tensor_copy(end_col, PS[0:E, 2, 0:1]))
            v.tensor_scalar(ended[:, :], K[0:E, C_TILE:C_TILE + TILES], end_col, None, ALU.is_ge).then_inc(cmp_ready, 1)
            dve.wait_ge(tab_mm, 1)
            L(v.scalar_tensor_tensor(rowf[:, 0, :], K[0:1, C_TILE:C_TILE + TILES], float(P), PS[0:1, 4, 0:TILES],
                                     ALU.mult, ALU.add))
            L(v.tensor_scalar(tab_row[:, :], rowf[:, 0, :], float(PAD0), None, ALU.min))
            v.tensor_scalar(tab_e[:, :], PS[0:1, 3, 0:TILES], float(E - 1), None, ALU.min).then_inc(tab_ready, 1)

            rest = cell[0][:, 0, :]
            mid_part = cell[0][:, 1, 0:FF].bitcast(bf16)
            dve.wait_ge(bias_in, 48)
            L(v.tensor_copy(bias_gu[:, :], bias_src[:, :]))
            L(v.tensor_tensor(rest, bias_src[:, :], bias_gu[:, :], ALU.subtract))
            L(v.tensor_copy(bias_gu[32:64, :], rest[32:64, :]))
            L(v.tensor_copy(mid_part, rest))
            L(v.tensor_tensor(rest, rest, mid_part, ALU.subtract))
            v.tensor_copy(bias_gu[64:96, :], rest[64:96, :]).then_inc(bias_done, 1)

            def tile(j, u):
                b = u % 2
                acc = PS[:, 2 + b, :]
                dve.wait_ge(gu_mm, j + 1)
                v.tensor_scalar(gate[b], acc[:, 0:FF], LIMIT, None, ALU.min).then_inc(gate_ready, 1)
                L(v.tensor_scalar(up[b], acc[:, FF:2 * FF], LIMIT, -LIMIT, ALU.min, ALU.max))
                dve.wait_ge(sg_ready, j + 1)
                L(v.scalar_tensor_tensor(glu[b], sg[b], 1.0, gate[b], ALU.add, ALU.mult))
                v.scalar_tensor_tensor(act_[b], up[b], 1.0, glu[b], ALU.add, ALU.mult).then_inc(act_ready, 1)

            with dve.Fori(0, TURNS) as i:
                L.start(i, 2 * UN)
                for u in range(UN):
                    tile(UN * i + u, u)
            L.stop(TURNS)

            def group(g, b):
                dve.wait_ge(zs_free, BT * g + (BT + 2))
                stats(lambda j: PS[:, 2 + 2 * b + j // 2, (j % 2) * DIM:(j % 2 + 1) * DIM], mv2, LN_EPS)
                newton(BT, rs[:, 0:BT])
                v.scalar_tensor_tensor(mr2, mv2[:, :, 0], -1.0, rs[:, 0:BT], ALU.mult, ALU.mult).then_inc(rz_ready, 1)

            def add_z(g, b):
                Xb = X[:, ds(BT * g, BT), :]
                dve.wait_ge(yz_ready, g + 3)
                v.tensor_tensor(Xb, Xb, yz[b], ALU.add).then_inc(yo_ready, 1)

            with dve.Fori(0, NBLK // 2) as i:
                L.start(i, 28)
                for b in range(2):
                    group(2 * i + b, b)
                    add_z(2 * i + b, b)
            L.stop(NBLK // 2)


def kernel(**inputs):
    import concourse.bacc as bacc
    from concourse.bass_utils import run_bass_kernel_spmd

    a = {n: np.asarray(inputs[n]) for n in inputs}

    def tiles_of(w):
        return np.ascontiguousarray(w.reshape(-1, P, w.shape[-1]).transpose(1, 0, 2))

    order = (3, 0, 1, 2)
    wg = a["L0_attn_W_gate"].reshape(PAIRS, 2, 4, HD, DIM)[:, :, order].transpose(2, 0, 1, 3, 4).reshape(GATES, DIM)
    bg = a["L0_attn_b_gate"].reshape(PAIRS, 2, 4, HD)[:, :, order].transpose(2, 0, 1, 3).reshape(CHUNKS, P)
    gu = a["L0_ffn_gate_up_proj"].reshape(E, KT, P, FF, 2).transpose(2, 0, 1, 4, 3)
    dn = a["L0_ffn_down_proj"].reshape(E, KT, P, DIM).transpose(2, 0, 1, 3)
    cst, cstb = constants()
    arrays = {
        "x": np.ascontiguousarray(a["L0_attn_x"].reshape(TOKENS, DIM)),
        "w_in": tiles_of(a["L0_attn_W_in"]),
        "w_gate": tiles_of(wg.T),
        "b_gate": np.ascontiguousarray(bg.T),
        "rms_w": np.ascontiguousarray(np.tile(a["L0_attn_rms_w"], 2).reshape(P, 1)),
        "w_out": tiles_of(a["L0_attn_W_out"].T),
        "w_router": tiles_of(a["L0_ffn_router_weight"].T),
        "b_router": np.ascontiguousarray(np.broadcast_to(a["L0_ffn_router_bias"], (P, E))),
        "w_gu": np.ascontiguousarray(gu).reshape(P, -1),
        "b_gu": np.ascontiguousarray(a["L0_ffn_gate_up_proj_bias"].reshape(E, FF, 2).transpose(0, 2, 1)).reshape(E, 2 * FF),
        "w_dn": np.ascontiguousarray(dn).reshape(P, -1),
        "b_dn": np.ascontiguousarray(a["L0_ffn_down_proj_bias"]),
        "cst": cst,
        "cstb": cstb,
    }
    nc = bacc.Bacc("TRN2", target_bir_lowering=False, num_devices=1)
    f32 = mybir.dt.float32
    args = [nc.dram_tensor(n, v.shape, f32, kind="ExternalInput").ap() for n, v in arrays.items()]
    out = nc.dram_tensor("out", [TOKENS, DIM], f32, kind="ExternalOutput").ap()
    build(nc, *args, out)
    r = run_bass_kernel_spmd(nc, [arrays], core_ids=[0])
    return r.results[0]["out"].reshape(BATCH, SEQ, DIM)
```

```python
import concourse.bass as bass
from concourse import mybir
from contextlib import ExitStack
import numpy as np

P = 128
BATCH, SEQ, DIM = 16, 256, 256
TOKENS = BATCH * SEQ
HEADS, HD = 4, 64
PAIRS = 2
KT = DIM // P
BLK = 512
BT = BLK // P
NBLK = TOKENS // BLK
NTILE = TOKENS // P
GATES = 4 * DIM
CHUNKS = GATES // P
E, TOPK, FF = 16, 4, 256
ROW = DIM + 2 * E
REGION = TOKENS + P
PAD0 = E * REGION
ZROWS = TOKENS * TOPK
TILES = -(-(ZROWS + E * (P - 1)) // P)
UN = 4
TURNS = -(-TILES // UN)
TILES = TURNS * UN
LIMIT, ALPHA = 7.0, 1.702
LN_EPS, RMS_EPS = 1e-5, 1e-6
MAGIC = float(0x5F3759DF)
PER_TURN = 96

C_IDENT, C_HALF, C_IOTA, C_BASE, C_DEST, C_SEL = 0, 128, 130, 146, 162, 178
C_TILE = C_SEL + 8 * P
C_TRI16 = C_TILE + TILES
C_PAD = C_TRI16 + E
C_DUMP = C_PAD + ROW
C_LEN = C_DUMP + UN
B_TRI, B_ONE, B_PICK = 0, 128, 256
B_LEN = B_PICK + E * P


def constants():
    c = np.zeros((P, C_LEN), np.float32)
    p = np.arange(P)
    c[:, C_IDENT:C_IDENT + P] = np.eye(P)
    c[:, C_HALF:C_HALF + 2] = (p[:, None] // HD) == np.arange(2)
    c[:, C_IOTA:C_IOTA + E] = np.arange(E)
    c[:, C_BASE:C_BASE + E] = np.arange(E) * REGION
    c[:, C_DEST:C_DEST + BT * TOPK] = (TOPK * (P * np.arange(BT)[None, :, None] + p[:, None, None])
                                       + np.arange(TOPK)).reshape(P, -1)
    for j in range(BT):
        for q in range(PAIRS):
            for half in range(2):
                lo = C_SEL + (j * PAIRS + q) * P + half * HD
                c[j * HEADS + 2 * q + half, lo:lo + HD] = 1.0
    c[:, C_TILE:C_TILE + TILES] = np.arange(TILES)
    c[:E, C_TRI16:C_TRI16 + E] = np.arange(E)[:, None] <= np.arange(E)
    c[:, C_PAD + DIM:C_PAD + DIM + E] = 2 * ZROWS
    c[:, C_DUMP:C_DUMP + UN] = ZROWS + P * np.arange(UN) + p[:, None]
    b = np.zeros((P, B_LEN), np.float32)
    b[:, B_TRI:B_TRI + P] = p[:, None] < p
    b[:, B_ONE:B_ONE + P] = 1.0
    for e in range(E):
        for part in range(3):
            b[32 * part + e, B_PICK + e * P:B_PICK + (e + 1) * P] = 1.0
    return c, b


class Link:

    def __init__(self, eng, sem):
        self.eng, self.sem, self.n, self.turn = eng, sem, 0, 0

    def __call__(self, ins, apart=False):
        ins.then_inc(self.sem, 1)
        self.n += 1
        self.eng.wait_ge(self.sem, self.n + self.turn)
        if apart:
            self.eng.nop(nofuse=True)

    def send(self, ins):
        ins.then_inc(self.sem, 1)
        self.n += 1
        return self.n + self.turn

    def wait(self, count):
        self.eng.wait_ge(self.sem, count)

    def start(self, i, per):
        self.turn, self.per, self.first = i * per, per, self.n

    def stop(self, turns):
        assert self.n - self.first == self.per, (self.n - self.first, self.per)
        self.n, self.turn = self.first + self.per * turns, 0


def build(nc, x, w_in, w_gate, b_gate, rms_w, w_out, w_router, b_router, w_gu, b_gu, w_dn, b_dn,
          cst, cstb, out):
    f32, bf16 = mybir.dt.float32, mybir.dt.bfloat16
    i32, u32 = mybir.dt.int32, mybir.dt.uint32
    ALU = mybir.AluOpType
    ACT = mybir.ActivationFunctionType
    AX = mybir.AxisListType.X
    ds = bass.ds

    ctx = ExitStack()
    with ctx:
        def sb(name, shape, dt=f32):
            return ctx.enter_context(nc.sbuf_tensor(name, shape, dt))

        def sem(name):
            return ctx.enter_context(nc.semaphore(name))

        routed = nc.dram_tensor("routed", [PAD0 + P, ROW], f32, kind="Internal").ap()
        expert_out = nc.dram_tensor("expert_out", [ZROWS + UN * P, DIM], f32, kind="Internal").ap()

        X = sb("X", [P, NTILE, DIM])
        Wgu = sb("Wgu", [P, E * KT * 2 * FF])
        Wdn = sb("Wdn", [P, E * KT * DIM])
        K = sb("K", [P, C_LEN])
        KB = sb("KB", [P, B_LEN], bf16)
        Wd = sb("Wd", [P, NTILE, E])
        bias_src = sb("bias_src", [P, 2 * FF])
        bias_gu = sb("bias_gu", [P, 2 * FF], bf16)
        Bdn = sb("Bdn", [E, DIM])
        tab_row = sb("tab_row", [1, TILES], i32)
        tab_e = sb("tab_e", [1, TILES], i32)
        tab_pad = sb("tab_pad", [1, E], i32)
        small = sb("small", [P, 1024])
        arena = sb("arena", [P, 13200])
        PS = ctx.enter_context(nc.psum_tensor("PS", [P, 8, 512], f32))

        KBf = Wgu[:, 0:B_LEN]
        ident = K[:, C_IDENT:C_IDENT + P]
        triB, oneB = KB[:, B_TRI:B_TRI + P], KB[:, B_ONE:B_ONE + P]

        at = [0]

        def cut(n, parts=P):
            lo = at[0]
            at[0] += n
            assert at[0] <= 13200
            return arena[0:parts, lo:lo + n]

        WcT = cut(KT * GATES).rearrange("p (k g) -> p k g", k=KT)
        WoT = cut(PAIRS * DIM).rearrange("p (k g) -> p k g", k=PAIRS)
        WrT = cut(KT * E).rearrange("p (k g) -> p k g", k=KT)
        xn = cut(BT * DIM).rearrange("p (j d) -> p j d", j=BT)
        xT = cut(KT * BLK).rearrange("p (k t) -> p k t", k=KT)
        g_i = cut(PAIRS * BLK).rearrange("p (k t) -> p k t", k=PAIRS)
        g_c = cut(PAIRS * BLK).rearrange("p (k t) -> p k t", k=PAIRS)
        stage = at[0]
        g_o = [cut(PAIRS * BLK).rearrange("p (k t) -> p k t", k=PAIRS) for _ in range(2)]
        cell = [cut(PAIRS * BLK).rearrange("p (k t) -> p k t", k=PAIRS) for _ in range(2)]
        WgT = arena[:, stage:stage + KT * GATES].rearrange("p (k g) -> p k g", k=KT)
        WiT = arena[:, stage + KT * GATES:stage + KT * GATES + KT * DIM].rearrange("p (k g) -> p k g", k=KT)
        csq, g_f = [Wgu[:, 14 * 1024 + n * 1024:15 * 1024 + n * 1024].rearrange("p (k t) -> p k t", k=PAIRS)
                    for n in range(2)]
        late = E * KT * DIM // 2
        cn, hT, yn, x2T = [Wdn[:, late + n * 1024:late + (n + 1) * 1024].rearrange("p (k t) -> p k t", k=k)
                           for n, k in enumerate((PAIRS, PAIRS, BT, KT))]
        rows = [cut(BT * ROW).rearrange("p (j d) -> p j d", j=BT) for _ in range(2)]
        at[0] = 0
        xg = [cut(ROW) for _ in range(UN)]
        xgT = [cut(DIM).rearrange("p (k t) -> p k t", k=KT) for _ in range(2)]
        gate = [cut(FF) for _ in range(2)]
        up = [cut(FF) for _ in range(2)]
        sg = [cut(FF) for _ in range(2)]
        glu = [cut(FF) for _ in range(2)]
        act_ = [cut(FF) for _ in range(2)]
        actT = [cut(FF).rearrange("p (k t) -> p k t", k=KT) for _ in range(2)]
        yb = [cut(DIM) for _ in range(UN)]
        dst = [cut(1).bitcast(u32) for _ in range(UN)]
        dstf = [cut(1) for _ in range(UN)]
        wgt = [cut(1) for _ in range(UN)]
        at[0] = 0
        zin = [cut(TOPK * DIM).rearrange("p (k d) -> p k d", k=TOPK) for _ in range(4)]
        zs = [cut(4 * DIM).rearrange("p (u k d) -> p u k d", u=2, k=2) for _ in range(2)]
        zz = [cut(2 * DIM).rearrange("p (u d) -> p u d", u=2) for _ in range(2)]
        sT = [cut(BT * P, E) for _ in range(2)]
        ws = [cut(BT * E).rearrange("p (j e) -> p j e", j=BT) for _ in range(2)]
        yz = [cut(BT * DIM).rearrange("p (j d) -> p j d", j=BT) for _ in range(2)]

        sat = [0]

        def tiny(n, dt=f32, parts=P):
            lo = sat[0]
            sat[0] += n
            assert sat[0] <= 1024
            v = small[0:parts, lo:lo + n]
            return v if dt == f32 else v.bitcast(dt)

        bG = tiny(CHUNKS)
        rmsw = tiny(1)
        bR = tiny(E)
        mv1 = tiny(NTILE * 2).rearrange("p (j s) -> p j s", s=2)
        r1 = tiny(NTILE)
        nv, na, nb_, ny = tiny(NTILE), tiny(NTILE), tiny(NTILE), tiny(NTILE)
        st2 = tiny(BT * 6).rearrange("p (j s) -> p j s", s=6)
        mv2 = tiny(BT * 2).rearrange("p (j s) -> p j s", s=2)
        mv3 = tiny(BT * 2).rearrange("p (j s) -> p j s", s=2)
        mr1 = tiny(NTILE)
        rs = tiny(BT + BT * HEADS)
        r2, mr2, mr3 = tiny(BT), tiny(BT), tiny(BT)
        rT = tiny(P, parts=BT * HEADS)
        top = tiny(BT * 8).rearrange("p (j s) -> p j s", s=8)
        topi = tiny(BT * 8, u32).rearrange("p (j s) -> p j s", s=8)
        logit = tiny(BT * E).rearrange("p (j s) -> p j s", s=E)
        topf = tiny(BT * TOPK).rearrange("p (j s) -> p j s", s=TOPK)
        wexp = tiny(BT * TOPK).rearrange("p (j s) -> p j s", s=TOPK)
        wsum = tiny(BT)
        dest = tiny(BT * TOPK).rearrange("p (j s) -> p j s", s=TOPK)
        slotf = tiny(BT * TOPK).rearrange("p (j s) -> p j s", s=TOPK)
        slot = [tiny(BT * TOPK, i32) for _ in range(2)]
        cnt_col, nt_col, dl_col, end_col = [tiny(1, parts=E) for _ in range(4)]
        cnt_i = tiny(1, i32, parts=E)
        oh = sb("oh", [P, BT, TOPK, E])
        prod = sb("prod", [P, BT, TOPK, E])
        slot_e = sb("slot_e", [P, BT, E])
        chosen = sb("chosen", [P, BT, E], bf16)
        before = sb("before", [P, E], bf16)
        mstep = sb("mstep", [P, E])
        ended = sb("ended", [E, TILES])
        rowf = sb("rowf", [1, 2, TILES])

        s_const, s_w, s_moe, s_gate = sem("s_const"), sem("s_w"), sem("s_moe"), sem("s_gate")
        s_x = [sem(f"s_x{b}") for b in range(2)]
        bias_zero, bias_in, bias_done = sem("bias_zero"), sem("bias_in"), sem("bias_done")
        wc_mm, wc_copy, half_b, kb_ready = sem("wc_mm"), sem("wc_copy"), sem("half_b"), sem("kb_ready")
        xn_ready, xT_mm, xT_ready = sem("xn_ready"), sem("xT_mm"), sem("xT_ready")
        gate_mm, gate_act, f_ready = sem("gate_mm"), sem("gate_act"), sem("f_ready")
        cell_ready, csq_ready, ms_mm = sem("cell_ready"), sem("csq_ready"), sem("ms_mm")
        rms_ready, rT_mm, rT_ready, rb_mm = sem("rms_ready"), sem("rT_mm"), sem("rT_ready"), sem("rb_mm")
        cn_ready, tanh_ready, h_ready = sem("cn_ready"), sem("tanh_ready"), sem("h_ready")
        y_mm, r2_ready, yn_ready = sem("y_mm"), sem("r2_ready"), sem("yn_ready")
        r1_ready, r3_ready = sem("r1_ready"), sem("r3_ready")
        x2_ready, x2T_mm, x2T_ready = sem("x2_ready"), sem("x2T_mm"), sem("x2T_ready")
        log_mm, wdiff, wexp_ready = sem("log_mm"), sem("wdiff"), sem("wexp_ready")
        chosen_ready, rank_mm, before_ready = sem("chosen_ready"), sem("rank_mm"), sem("before_ready")
        slot_ready = sem("slot_ready")
        rows_sent = [sem(f"rows_sent{b}") for b in range(2)]
        rows_free = sem("rows_free")
        v_link = sem("v_link")
        cnt_mm, nt_ready, end_mm, cmp_ready = sem("cnt_mm"), sem("nt_ready"), sem("end_mm"), sem("cmp_ready")
        tab_mm, tab_ready, pad_sent = sem("tab_mm"), sem("tab_ready"), sem("pad_sent")
        xg_in = [sem(f"xg_in{u}") for u in range(UN)]
        tr_mm, tr_ready, gu_mm = sem("tr_mm"), sem("tr_ready"), sem("gu_mm")
        gate_ready, sg_ready, act_ready = sem("gate_ready"), sem("sg_ready"), sem("act_ready")
        aT_mm, aT_ready, y2_mm = sem("aT_mm"), sem("aT_ready"), sem("y2_mm")
        y2_ready = sem("y2_ready")
        dst_copied, dst_ready = sem("dst_copied"), sem("dst_ready")
        y_sent = [sem(f"y_sent{u}") for u in range(UN)]
        z_in = [sem(f"z_in{u}") for u in range(4)]
        zs_ready, zs_free = sem("zs_ready"), sem("zs_free")
        zz_ready, zz_free = sem("zz_ready"), sem("zz_free")
        sT_mm, sT_ready = sem("sT_mm"), sem("sT_ready")
        rz_ready, yz_ready, yo_ready = sem("rz_ready"), sem("yz_ready"), sem("yo_ready")
        out_sent, ws_ready = sem("out_sent"), sem("ws_ready")

        block = ctx.enter_context(nc.Block())
        x_v = x.rearrange("(n p) d -> p n d", p=P)
        out_v = out.rearrange("(n p) d -> p n d", p=P)

        def steps(eng, step, link=None, per=0):
            step(0, 0), step(1, 1)
            turns = (NBLK - 3) // 2
            with eng.Fori(0, turns) as i:
                if link:
                    link.start(i, per)
                step(2 * i + 2, 2, i)
                step(2 * i + 3, 3, i)
            if link:
                link.stop(turns)
            for s in range(2 + 2 * turns, NBLK + 2):
                step(s, s)

        def tiles(eng, step):
            for j in range(UN + 2):
                step(j, j)
            with eng.Fori(0, TURNS - 2) as i:
                for u in range(UN):
                    step(UN * i + (UN + 2 + u), UN + 2 + u, i)
            for j in range(TILES - 2, TILES + 2):
                step(j, j)

        def on(s0, lag):
            return 0 <= s0 - lag < NBLK

        @block.sync
        def _(sp):
            sp.sem_inc(rows_free, 2)
            sp.sem_inc(zs_free, 2)
            sp.sem_inc(zz_free, 2)
            sp.sem_inc(y2_ready, 2)
            sp.sem_inc(yz_ready, 2)
            def load_x(b):
                sp.dma_start(X[:, BT * b:BT * (b + 1), :], x_v[:, BT * b:BT * (b + 1), :]).then_inc(s_x[b % 2], 16)

            sp.dma_start(WiT, w_in).then_inc(s_gate, 16)
            sp.dma_start(WgT, w_gate).then_inc(s_gate, 16)
            load_x(0)
            sp.dma_start(K[:, :], cst).then_inc(s_const, 16)
            load_x(1)
            sp.dma_start(KBf, cstb).then_inc(s_const, 16)
            sp.dma_start(WoT, w_out).then_inc(s_w, 16)
            sp.dma_start(WrT, w_router).then_inc(s_w, 16)
            sp.dma_start(bG, b_gate).then_inc(s_w, 16)
            sp.dma_start(rmsw, rms_w).then_inc(s_w, 16)
            sp.dma_start(bR, b_router).then_inc(s_w, 16)
            for b in range(2, NBLK):
                sp.wait_ge(s_x[b % 2], 16 * (b // 2))
                load_x(b)
            sp.dma_start(Bdn[:, :], b_dn).then_inc(s_moe, 16)
            sp.wait_ge(kb_ready, 1)
            q = E * KT * 2 * FF // 8
            for n in range(7):
                sp.dma_start(Wgu[:, n * q:(n + 1) * q], w_gu[:, n * q:(n + 1) * q]).then_inc(s_moe, 16)
            q = E * KT * DIM // 4
            for n in range(2):
                sp.dma_start(Wdn[:, n * q:(n + 1) * q], w_dn[:, n * q:(n + 1) * q]).then_inc(s_moe, 16)
            sp.wait_ge(bias_zero, 1)
            for part in range(3):
                sp.dma_start(bias_src[32 * part:32 * part + E, :], b_gu).then_inc(bias_in, 16)
            sp.wait_ge(before_ready, NBLK + 1)
            sp.dma_start(Wgu[:, 14 * 1024:], w_gu[:, 14 * 1024:]).then_inc(s_moe, 16)
            for n in range(2, 4):
                sp.dma_start(Wdn[:, n * q:(n + 1) * q], w_dn[:, n * q:(n + 1) * q]).then_inc(s_moe, 16)

            sp.wait_ge(tab_ready, 1)
            pad = K[:, C_PAD:C_PAD + ROW]
            for e in range(E):
                first = sp.value_load(tab_pad[0:1, e:e + 1], min_val=e * REGION, max_val=e * REGION + TOKENS)
                sp.dma_start(routed[ds(first, P), :], pad).then_inc(pad_sent, 16)
            sp.dma_start(routed[PAD0:PAD0 + P, :], pad).then_inc(pad_sent, 16)
            sp.wait_ge(pad_sent, 16 * (E + 1))
            for b in range(2):
                sp.wait_ge(rows_sent[b], 16 * BT * TOPK * NBLK // 2)

            def load_tile(j, u):
                r = sp.value_load(tab_row[0:1, ds(j, 1)], min_val=0, max_val=PAD0)
                sp.dma_start(xg[u], routed[ds(r, P), :]).then_inc(xg_in[u], 16)

            for u in range(UN):
                load_tile(u, u)
            with sp.Fori(1, TURNS) as i:
                for u in range(UN):
                    sp.wait_ge(tr_mm, UN * i + (u + 1 - UN))
                    sp.wait_ge(dst_ready, UN * i + (u + 1 - UN))
                    load_tile(UN * i + u, u)

            for u in range(UN):
                sp.wait_ge(y_sent[u], 16 * TURNS)
            z_v = expert_out[0:ZROWS, :].rearrange("(n p k) d -> n p k d", p=P, k=TOPK)

            def load_z(n, u):
                sp.dma_start(zin[u], z_v[ds(n, 1), :, :, :].rearrange("n p k d -> (n p) k d")).then_inc(z_in[u], 16)

            for u in range(4):
                load_z(u, u)
            with sp.Fori(1, NTILE // 4) as i:
                for u in range(4):
                    sp.wait_ge(zs_ready, 4 * i + (u + 1 - 4))
                    load_z(4 * i + u, u)
            sp.wait_ge(out_sent, 16 * NBLK)

        @block.tensor
        def _(pe):
            mm = nc.tensor.matmul

            pe.wait_ge(s_gate, 16 * 2)
            for n in range(2):
                for m in range(KT):
                    for k in range(KT):
                        last = mm(PS[:, 2 * n + m, :], WiT[:, k, m * P:(m + 1) * P],
                                  WgT[:, k, n * 512:(n + 1) * 512], start=(k == 0), stop=(k == KT - 1))
                    last.then_inc(wc_mm, 1)

            def transposes_x(t):
                pe.wait_ge(xn_ready, t + 1)
                for k in range(KT):
                    for j in range(BT):
                        last = nc.tensor.transpose(PS[:, k, j * P:(j + 1) * P], xn[:, j, k * P:(k + 1) * P], ident)
                    last.then_inc(xT_mm, 1)

            def gates(t, c, first):
                if c == 0:
                    pe.wait_ge(xT_ready, 2 * t + 2)
                if first or c >= 2:
                    pe.wait_ge(gate_act, 8 * t + (c - 1))
                for k in range(KT):
                    last = mm(PS[:, 2 + c % 2, :], WcT[:, k, c * P:(c + 1) * P], xT[:, k, :],
                              start=(k == 0), stop=(k == KT - 1))
                last.then_inc(gate_mm, 1)

            def mean_square(t):
                pe.wait_ge(csq_ready, t + 1)
                for j in range(BT):
                    for q in range(PAIRS):
                        last = mm(PS[:, 6, HEADS * j + 2 * q:HEADS * j + 2 * q + 2], csq[:, q, j * P:(j + 1) * P],
                                  K[:, C_HALF:C_HALF + 2], start=True, stop=True)
                last.then_inc(ms_mm, 1)

            def rms_transpose(t):
                pe.wait_ge(rms_ready, t + 1)
                nc.tensor.transpose(PS[0:BT * HEADS, 6, P:2 * P], rs[:, BT:BT + BT * HEADS], ident).then_inc(rT_mm, 1)

            def rms_spread(t, later):
                pe.wait_ge(rT_ready, t + 1)
                if later:
                    pe.wait_ge(yn_ready, t)
                for q in range(PAIRS):
                    for j in range(BT):
                        lo = C_SEL + (j * PAIRS + q) * P
                        last = mm(PS[:, 4 + q, j * P:(j + 1) * P], K[0:BT * HEADS, lo:lo + P], rT,
                                  start=True, stop=True)
                last.then_inc(rb_mm, 1)

            def out_product(t):
                pe.wait_ge(h_ready, t + 1)
                for j in range(BT):
                    for q in range(PAIRS):
                        last = mm(PS[:, 4 + j // 2, (j % 2) * DIM:(j % 2 + 1) * DIM], hT[:, q, j * P:(j + 1) * P],
                                  WoT[:, q, :], start=(q == 0), stop=(q == PAIRS - 1))
                last.then_inc(y_mm, 1)

            def transposes_x2(t, rw):
                pe.wait_ge(x2_ready, t + 1)
                for k in range(KT):
                    for j in range(BT):
                        last = nc.tensor.transpose(PS[:, k, j * P:(j + 1) * P], rw[:, j, k * P:(k + 1) * P], ident)
                    last.then_inc(x2T_mm, 1)

            def logits(t):
                pe.wait_ge(x2T_ready, 2 * t + 2)
                for j in range(BT):
                    for k in range(KT):
                        last = mm(PS[:, 7, E * j:E * (j + 1)], x2T[:, k, j * P:(j + 1) * P], WrT[:, k, :],
                                  start=(k == 0), stop=(k == KT - 1))
                last.then_inc(log_mm, 1)

            def ranks(t):
                pe.wait_ge(chosen_ready, t + 1)
                pe.wait_ge(before_ready, t + 1)
                R = PS[:, 7, 256:256 + BT * E].rearrange("p (j e) -> p j e", e=E)
                mm(R, triB, chosen[:, :, :], start=True, stop=False)
                mm(R, oneB, before[:, :].unsqueeze(1).to_broadcast([P, BT, E]), start=False, stop=False)
                for j in range(BT - 1):
                    last = mm(R[:, j + 1:BT, :], oneB,
                              chosen[:, j:j + 1, :].to_broadcast([P, BT - 1 - j, E]),
                              start=False, stop=(j == BT - 2))
                last.then_inc(rank_mm, 1)

            def step(s, s0, i=None):
                new, mid, old = on(s0, 0), on(s0, 1), on(s0, 2)
                for c in range(CHUNKS):
                    if new:
                        gates(s, c, s0 > 0)
                    if c == 2 and mid:
                        mean_square(s - 1)
                    if c == 3 and mid:
                        rms_transpose(s - 1)
                    if c == 4 and mid:
                        rms_spread(s - 1, s0 > 1)
                    if c == 4 and old:
                        transposes_x2(s - 2, rows[s0 % 2])
                    if c == 5 and old:
                        logits(s - 2)
                    if c == 5 and mid:
                        out_product(s - 1)
                    if c == 6 and old:
                        ranks(s - 2)
                if on(s0, -1):
                    transposes_x(s + 1)

            pe.wait_ge(s_const, 32)
            pe.wait_ge(s_w, 16 * 5)
            pe.wait_ge(wc_copy, 4)
            transposes_x(0)
            pe.wait_ge(kb_ready, 1)
            steps(pe, step)

            pe.wait_ge(before_ready, NBLK + 1)
            mm(PS[0:1, 0, 0:E], KB[:, B_ONE:B_ONE + 1], before[:, :], start=True, stop=True)
            mm(PS[0:E, 1, 0:1], before[:, :], KB[:, B_ONE:B_ONE + 1], start=True, stop=True).then_inc(cnt_mm, 1)
            pe.wait_ge(nt_ready, 1)
            mm(PS[0:E, 2, 0:1], K[0:E, C_TRI16:C_TRI16 + E], nt_col, start=True, stop=True).then_inc(end_mm, 1)
            pe.wait_ge(cmp_ready, 1)
            mm(PS[0:1, 3, 0:TILES], K[0:E, C_TRI16 + E - 1:C_TRI16 + E], ended[:, :], start=True, stop=True)
            mm(PS[0:1, 4, 0:TILES], dl_col, ended[:, :], start=True, stop=True).then_inc(tab_mm, 1)

            pe.wait_ge(s_moe, 16 * 13)
            pe.wait_ge(bias_done, 1)
            pe.wait_ge(tab_ready, 1)

            def tile_transposes(j, uj, i):
                pe.wait_ge(xg_in[uj % UN], 16 * (uj // UN + 1) if i is None else 16 * i + 16 * (uj // UN + 1))
                for k in range(KT):
                    last = nc.tensor.transpose(PS[:, uj % 2, k * P:(k + 1) * P],
                                               xg[uj % UN][:, k * P:(k + 1) * P], ident)
                last.then_inc(tr_mm, 1)

            def gate_up(j, uj):
                e = pe.value_load(tab_e[0:1, ds(j, 1)], min_val=0, max_val=E - 1)
                acc = PS[:, 2 + uj % 2, :]
                mm(acc, KB[:, ds(e * P + B_PICK, P)], bias_gu[:, :], start=True, stop=False)
                pe.wait_ge(tr_ready, j + 1)
                for k in range(KT):
                    last = mm(acc, xgT[uj % 2][:, k, :], Wgu[:, ds(e * (KT * 2 * FF) + k * 2 * FF, 2 * FF)],
                              start=False, stop=(k == KT - 1))
                last.then_inc(gu_mm, 1)

            def act_transposes(j, uj):
                pe.wait_ge(act_ready, j + 1)
                for k in range(KT):
                    last = nc.tensor.transpose(PS[:, 4 + uj % 2, k * P:(k + 1) * P],
                                               act_[uj % 2][:, k * P:(k + 1) * P], ident)
                last.then_inc(aT_mm, 1)

            def down(j, uj):
                e = pe.value_load(tab_e[0:1, ds(j, 1)], min_val=0, max_val=E - 1)
                pe.wait_ge(y2_ready, j + 1)
                pe.wait_ge(aT_ready, j + 1)
                for k in range(KT):
                    last = mm(PS[:, 6 + uj % 2, 0:DIM], actT[uj % 2][:, k, :],
                              Wdn[:, ds(e * (KT * DIM) + k * DIM, DIM)], start=(k == 0), stop=(k == KT - 1))
                last.then_inc(y2_mm, 1)

            def tile_step(j, uj, i=None):
                if uj < 2:
                    if uj == 0:
                        tile_transposes(0, 0, None)
                    tile_transposes(j + 1, uj + 1, None)
                    gate_up(j, uj)
                    return
                act_transposes(j - 2, uj - 2)
                if i is not None or j + 1 < TILES:
                    tile_transposes(j + 1, uj + 1, i)
                if i is not None or j < TILES:
                    gate_up(j, uj)
                down(j - 2, uj - 2)

            tiles(pe, tile_step)

            def transpose_weights(g, b):
                pe.wait_ge(ws_ready, g + 1)
                for u in range(BT):
                    last = nc.tensor.transpose(PS[0:E, b, u * P:(u + 1) * P], ws[b][:, u, :], ident)
                last.then_inc(sT_mm, 1)

            def combine(g, b, more=True):
                pe.wait_ge(sT_ready, g + 1)
                pe.wait_ge(yz_ready, g + 1)
                for h in range(2):
                    for u in range(2):
                        mm(PS[:, 2 + 2 * b + h, u * DIM:(u + 1) * DIM], sT[b][:, (2 * h + u) * P:(2 * h + u + 1) * P],
                           Bdn[:, :], start=(u == 0), stop=False)
                if more:
                    transpose_weights(g + 1, 1 - b)
                for h in range(2):
                    pe.wait_ge(zz_ready, 2 * g + (h + 1))
                    mm(PS[:, 2 + 2 * b + h, :], ident, zz[h], start=False, stop=True).then_inc(zz_free, 1)

            transpose_weights(0, 0)
            with pe.Fori(0, NBLK // 2 - 1) as i:
                for b in range(2):
                    combine(2 * i + b, b)
            combine(NBLK - 2, 0)
            combine(NBLK - 1, 1, False)

        @block.scalar
        def _(act):
            def copy(o, i, **kw):
                return nc.scalar.activation(o, i, ACT.Copy, **kw)

            for n in range(2):
                for m in range(KT):
                    act.wait_ge(wc_mm, 2 * n + m + 1)
                    copy(WcT[:, m, n * 512:(n + 1) * 512], PS[:, 2 * n + m, :]).then_inc(wc_copy, 1)

            def evac_x(t):
                for k in range(KT):
                    act.wait_ge(xT_mm, 2 * t + (k + 1))
                    copy(xT[:, k, :], PS[:, k, :]).then_inc(xT_ready, 1)

            def gate_chunk(t, c, s0):
                kind, q = c // 2, c % 2
                if c == 0 and s0 >= 1:
                    act.wait_ge(cell_ready, t)
                if c == 6 and s0 >= 2:
                    act.wait_ge(h_ready, t - 1)
                act.wait_ge(gate_mm, 8 * t + (c + 1))
                nc.scalar.activation((g_c, g_i, g_f, g_o[s0 % 2])[kind][:, q, :], PS[:, 2 + c % 2, :],
                                     ACT.Exp if kind == 1 else ACT.Tanh, bias=bG[:, c:c + 1],
                                     scale=1.0 if kind < 2 else 0.5).then_inc(gate_act, 1)
                if c == 5:
                    act.wait_ge(gate_act, 8 * t + 6)
                    copy(g_f, g_f, bias=0.5, scale=0.5).then_inc(f_ready, 1)

            def norm_x(t):
                for j in range(BT):
                    n = ds(BT * t + j, 1)
                    last = nc.scalar.activation(xn[:, j, :], X[:, n, :].rearrange("p n d -> p (n d)"), ACT.Identity,
                                                bias=mr1[:, n], scale=r1[:, n])
                last.then_inc(xn_ready, 1)

            def norm_x1(t, par):
                act.wait_ge(r3_ready, t + 1)
                act.wait_ge(rows_free, t + 1)
                for j in range(BT):
                    last = nc.scalar.activation(rows[par][:, j, 0:DIM],
                                                X[:, ds(BT * t + j, 1), :].rearrange("p n d -> p (n d)"),
                                                ACT.Identity, bias=mr3[:, j:j + 1], scale=rs[:, j:j + 1])
                last.then_inc(x2_ready, 1)

            def square(t, par, later):
                act.wait_ge(cell_ready, t + 1)
                if later:
                    act.wait_ge(ms_mm, t)
                nc.scalar.activation(csq, cell[par], ACT.Square).then_inc(csq_ready, 1)

            def rms_row(t):
                act.wait_ge(rT_mm, t + 1)
                copy(rT, PS[0:BT * HEADS, 6, P:2 * P]).then_inc(rT_ready, 1)

            def tanh_c(t):
                act.wait_ge(cn_ready, t + 1)
                nc.scalar.activation(cn, cn, ACT.Tanh, scale=rmsw).then_inc(tanh_ready, 1)

            def norm_y(t):
                act.wait_ge(r2_ready, t + 1)
                for j in range(BT):
                    last = nc.scalar.activation(yn[:, j, :], PS[:, 4 + j // 2, (j % 2) * DIM:(j % 2 + 1) * DIM],
                                                ACT.Identity, bias=mr2[:, j:j + 1], scale=r2[:, j:j + 1])
                last.then_inc(yn_ready, 1)

            def evac_x2(t):
                for k in range(KT):
                    act.wait_ge(x2T_mm, 2 * t + (k + 1))
                    copy(x2T[:, k, :], PS[:, k, :]).then_inc(x2T_ready, 1)

            def weights_exp(t):
                act.wait_ge(wdiff, t + 1)
                nc.scalar.activation(wexp, wexp, ACT.Exp).then_inc(wexp_ready, 1)

            def step(s, s0, i=None):
                new, mid, old = on(s0, 0), on(s0, 1), on(s0, 2)
                for c in range(CHUNKS):
                    if c == 1 and mid:
                        square(s - 1, (s0 - 1) % 2, s0 > 1)
                    if new:
                        gate_chunk(s, c, s0)
                    if c == 3 and mid:
                        rms_row(s - 1)
                    if c == 3 and old:
                        norm_x1(s - 2, s0 % 2)
                    if c == 4 and mid:
                        tanh_c(s - 1)
                    if c == 4 and old:
                        evac_x2(s - 2)
                    if c == 5 and on(s0, -1):
                        if s0 == 0:
                            act.wait_ge(r1_ready, 2)
                        norm_x(s + 1)
                    if c == 5 and old:
                        weights_exp(s - 2)
                if on(s0, -1):
                    evac_x(s + 1)
                if mid:
                    norm_y(s - 1)

            act.wait_ge(r1_ready, 1)
            norm_x(0)
            evac_x(0)
            act.wait_ge(half_b, 1)
            steps(act, step)

            def evac_tile(j, uj):
                act.wait_ge(tr_mm, j + 1)
                copy(xgT[uj % 2], PS[:, uj % 2, 0:DIM].rearrange("p (k t) -> p k t", k=KT)).then_inc(tr_ready, 1)

            def tile_step(j, uj, i=None):
                running = i is not None
                if uj == 0:
                    evac_tile(0, 0)
                if uj >= 2:
                    act.wait_ge(aT_mm, j - 1)
                    copy(actT[uj % 2], PS[:, 4 + uj % 2, 0:FF].rearrange("p (k t) -> p k t", k=KT)).then_inc(aT_ready, 1)
                if running or j + 1 < TILES:
                    evac_tile(j + 1, uj + 1)
                if running or j < TILES:
                    act.wait_ge(gate_ready, j + 1)
                    nc.scalar.activation(sg[uj % 2], gate[uj % 2], ACT.Tanh, scale=ALPHA / 2).then_inc(sg_ready, 1)
                if uj >= 2:
                    u = (uj - 2) % UN
                    act.wait_ge(dst_ready, j - 1)
                    if uj - 2 >= UN:
                        turn = (uj - 2) // UN
                        act.wait_ge(y_sent[u], 16 * i + 16 * turn if running else 16 * turn)
                    act.wait_ge(y2_mm, j - 1)
                    copy(yb[u], PS[:, 6 + uj % 2, 0:DIM], scale=wgt[u]).then_inc(y2_ready, 1)

            tiles(act, tile_step)

            for u in range(UN):
                act.wait_ge(y_sent[u], 16 * TURNS)

            def store(g):
                act.wait_ge(yo_ready, g + 1)
                act.dma_start(out_v[:, ds(BT * g, BT), :], X[:, ds(BT * g, BT), :]).then_inc(out_sent, 16)

            def stage_weights(g, b):
                copy(ws[b], Wd[:, ds(BT * g, BT), :]).then_inc(ws_ready, 1)

            def evac_weights(g, b):
                act.wait_ge(sT_mm, g + 1)
                copy(sT[b], PS[0:E, b, :]).then_inc(sT_ready, 1)

            def group(g, b, first=False, ahead=2):
                if ahead > 0:
                    evac_weights(g + 1, 1 - b)
                if ahead > 1:
                    stage_weights(g + 2, b)
                act.wait_ge(rz_ready, g + 1)
                for u in range(BT):
                    last = nc.scalar.activation(yz[b][:, u, :], PS[:, 2 + 2 * b + u // 2, (u % 2) * DIM:(u % 2 + 1) * DIM],
                                                ACT.Identity, bias=mr2[:, u:u + 1], scale=r2[:, u:u + 1])
                last.then_inc(yz_ready, 1)
                if not first:
                    store(g - 1)

            stage_weights(0, 0)
            stage_weights(1, 1)
            evac_weights(0, 0)
            group(0, 0, True)
            group(1, 1)
            with act.Fori(1, NBLK // 2 - 1) as i:
                group(2 * i, 0)
                group(2 * i + 1, 1)
            group(NBLK - 2, 0, ahead=1)
            group(NBLK - 1, 1, ahead=0)
            store(NBLK - 1)

        @block.gpsimd
        def _(pool):
            def wait(s, n):
                pool.wait_ge(s, n)
                if not isinstance(n, int):
                    pool.nop(nofuse=True)

            def step(s, s0, i=None):
                if on(s0, 2):
                    wait(slot_ready, s - 1)
                    for jk in range(BT * TOPK):
                        idx = slot[s0 % 2][:, jk:jk + 1].bitcast(u32)
                        pool.indirect_dma_start(routed, bass.IndirectOffsetOnAxis(ap=idx, axis=0),
                                                rows[s0 % 2][:, jk // TOPK, :], None).then_inc(rows_sent[s0 % 2], 16)
                    n = 16 * BT * TOPK
                    pool.wait_ge(rows_sent[s0 % 2], n * (s0 // 2) if i is None else n * i + n * (s0 // 2))
                    pool.sem_inc(rows_free, 1)

            steps(pool, step)

            pool.wait_ge(tab_ready, 1)

            def tile_step(j, uj, i=None):
                running = i is not None
                if uj >= 2:
                    u = (uj - 2) % UN
                    wait(y2_ready, j + 1)
                    pool.indirect_dma_start(expert_out, bass.IndirectOffsetOnAxis(ap=dst[u], axis=0),
                                            yb[u], None).then_inc(y_sent[u], 16)
                if running or j < TILES:
                    u = uj % UN
                    e = pool.value_load(tab_e[0:1, ds(j, 1)], min_val=0, max_val=E - 1)
                    turn = uj // UN
                    if turn:
                        wait(y_sent[u], 16 * i + 16 * turn if running else 16 * turn)
                    wait(xg_in[u], 16 * i + (16 + 16 * turn) if running else 16 + 16 * turn)
                    pool.tensor_copy(wgt[u], xg[u][:, ds(e + (DIM + E), 1)])
                    pool.tensor_copy(dstf[u], xg[u][:, ds(e + DIM, 1)]).then_inc(dst_copied, 1)
                    wait(dst_copied, j + 1)
                    pool.tensor_scalar(dst[u], dstf[u], K[:, C_DUMP + u:C_DUMP + u + 1], None,
                                       ALU.min).then_inc(dst_ready, 1)

            tiles(pool, tile_step)

            def pair_sums(n, u, i):
                wait(z_in[u], 16 * i + 16)
                if u % 2 == 0:
                    wait(zs_free, 2 * i + (u // 2 + 1))
                pool.tensor_tensor(zs[u // 2][:, u % 2], zin[u][:, 0:2, :], zin[u][:, 2:4, :], ALU.add).then_inc(zs_ready, 1)

            with pool.Fori(0, NTILE // 4) as i:
                for u in range(4):
                    pair_sums(4 * i + u, u, i)

        @block.vector
        def _(dve):
            v = nc.vector
            L = Link(dve, v_link)

            def newton(w, o, last=None):
                a, b, y, s = na[:, 0:w], nb_[:, 0:w], ny[:, 0:w], nv[:, 0:w]
                L(v.tensor_scalar(a.bitcast(i32), s.bitcast(i32), 1, None, ALU.logical_shift_right))
                L(v.tensor_scalar(y.bitcast(i32), a.bitcast(i32), -1.0, MAGIC, ALU.mult, ALU.add))
                for n in range(3):
                    L(v.tensor_tensor(a, y, y, ALU.mult))
                    L(v.scalar_tensor_tensor(b, a, -0.5, s, ALU.mult, ALU.mult))
                    (last if last and n == 2 else L)(
                        v.scalar_tensor_tensor(y if n < 2 else o, b, 1.5, y, ALU.add, ALU.mult))

            v.memset(bias_src[:, :], 0.0).then_inc(bias_zero, 1)
            v.memset(before[:, :], 0.0).then_inc(before_ready, 1)

            def stats_x(place):
                for j in range(BT):
                    last = v.bn_stats(st2[:, j, :], X[:, ds(place + j, 1), :].rearrange("p n d -> p (n d)"))
                L(last, True)
                for j in range(BT):
                    last = v.bn_aggr(mv2[:, j, :], st2[:, j, :])
                L(last)
                L(v.tensor_copy(mv1[:, ds(place, BT), :], mv2))

            def norms_x(lo, hi):
                L(v.tensor_scalar(nv[:, 0:hi - lo], mv1[:, lo:hi, 1], LN_EPS, None, ALU.add))
                newton(hi - lo, r1[:, lo:hi])
                v.scalar_tensor_tensor(mr1[:, lo:hi], mv1[:, lo:hi, 0], -1.0, r1[:, lo:hi], ALU.mult,
                                       ALU.mult).then_inc(r1_ready, 1)

            dve.wait_ge(s_x[0], 16)
            stats_x(0)
            norms_x(0, BT)
            dve.wait_ge(s_w, 16 * 5)
            v.tensor_scalar(bG[:, 4:8], bG[:, 4:8], 0.5, None, ALU.mult).then_inc(half_b, 1)
            dve.wait_ge(s_const, 32)
            v.tensor_copy(KB[:, :], KBf).then_inc(kb_ready, 1)
            L(v.tensor_copy(dest, K[:, C_DEST:C_DEST + BT * TOPK].rearrange("p (j k) -> p j k", k=TOPK)))
            dve.wait_ge(s_x[1], 16)
            stats_x(BT)
            with dve.Fori(1, NBLK // 2) as i:
                L.start(i - 1, 6)
                for b in range(2):
                    dve.wait_ge(s_x[b], 16 * i + 16)
                    dve.nop(nofuse=True)
                    stats_x(2 * BT * i + BT * b)
            L.stop(NBLK // 2 - 1)
            norms_x(BT, NTILE)

            def scan(t, par):
                dve.wait_ge(gate_act, 8 * t + 4)
                L(v.tensor_tensor(g_i, g_i, g_c, ALU.mult))
                dve.wait_ge(f_ready, t + 1)
                for q in range(PAIRS):
                    for b in range(BLK // SEQ):
                        w = slice(b * SEQ, (b + 1) * SEQ)
                        last = v.tensor_tensor_scan(cell[par][:, q, w], g_f[:, q, w], g_i[:, q, w], 0.0,
                                                    ALU.mult, ALU.add)
                last.then_inc(cell_ready, 1)

            def stats(src, mv, eps):
                dve.nop(nofuse=True)
                for j in range(BT):
                    last = v.bn_stats(st2[:, j, :], src(j))
                L(last, True)
                for j in range(BT):
                    last = v.bn_aggr(mv[:, j, :], st2[:, j, :])
                L(last)
                L(v.tensor_scalar(nv[:, 0:BT], mv[:, :, 1], eps, None, ALU.add))

            def residual(t):
                Xb = X[:, ds(BT * t, BT), :]
                dve.wait_ge(yn_ready, t + 1)
                L(v.tensor_tensor(Xb, Xb, yn, ALU.add))
                stats(lambda j: X[:, ds(BT * t + j, 1), :].rearrange("p n d -> p (n d)"), mv3, LN_EPS)

            def block_norms(t, mid, old):
                if not old:
                    L(v.memset(nv[:, 0:BT], 1.0))
                if mid:
                    dve.wait_ge(ms_mm, t + 1)
                    L(v.tensor_scalar(nv[:, BT:BT + BT * HEADS], PS[:, 6, 0:BT * HEADS], 1.0 / HD, RMS_EPS,
                                      ALU.mult, ALU.add))

                    def done(ins):
                        ins.then_inc(rms_ready, 1)
                        dve.wait_ge(rms_ready, t + 1)
                    newton(BT + BT * HEADS, rs, done)
                else:
                    newton(BT, rs[:, 0:BT])
                if old:
                    v.scalar_tensor_tensor(mr3, mv3[:, :, 0], -1.0, rs[:, 0:BT], ALU.mult, ALU.mult).then_inc(r3_ready, 1)

            def y_stats(t):
                dve.wait_ge(y_mm, t + 1)
                stats(lambda j: PS[:, 4 + j // 2, (j % 2) * DIM:(j % 2 + 1) * DIM], mv2, 4 * LN_EPS)

            def y_norm(done=r2_ready):
                a, b, y, x = na[:, 0:BT], nb_[:, 0:BT], ny[:, 0:BT], nv[:, 0:BT]
                n = L.send(v.tensor_scalar(a.bitcast(i32), x.bitcast(i32), 1, None, ALU.logical_shift_right))
                yield
                L.wait(n)
                n = L.send(v.tensor_scalar(y.bitcast(i32), a.bitcast(i32), -1.0, MAGIC, ALU.mult, ALU.add))
                for turn in range(3):
                    yield
                    L.wait(n)
                    n = L.send(v.tensor_tensor(a, y, y, ALU.mult))
                    yield
                    L.wait(n)
                    n = L.send(v.scalar_tensor_tensor(b, a, -0.5, x, ALU.mult, ALU.mult))
                    yield
                    L.wait(n)
                    n = L.send(v.scalar_tensor_tensor(r2 if turn == 2 else y, b, 1.5, y, ALU.add, ALU.mult))
                yield
                L.wait(n)
                v.scalar_tensor_tensor(mr2, mv2[:, :, 0], -1.0, r2, ALU.mult, ALU.mult).then_inc(done, 1)

            def scale_cell(t, par):
                dve.wait_ge(rb_mm, t + 1)
                v.tensor_tensor(cn, cell[par], PS[:, 4:6, :], ALU.mult).then_inc(cn_ready, 1)

            def hidden(t, par):
                dve.wait_ge(tanh_ready, t + 1)
                v.scalar_tensor_tensor(hT, g_o[par], 1.0, cn, ALU.add, ALU.mult).then_inc(h_ready, 1)

            JK = [P, BT, TOPK, E]

            def choose(t, par):
                dve.wait_ge(log_mm, t + 1)
                L(v.tensor_tensor(logit, PS[:, 7, 0:BT * E].rearrange("p (j e) -> p j e", e=E),
                                  bR.unsqueeze(1).to_broadcast([P, BT, E]), ALU.add), True)
                for j in range(BT):
                    last = v.max(top[:, j, :], logit[:, j, :])
                L(last, True)
                for j in range(BT):
                    last = v.max_index(topi[:, j, :], top[:, j, :], logit[:, j, :])
                L(last)
                v.tensor_tensor(wexp, top[:, :, 0:TOPK], top[:, :, 0:1].to_broadcast([P, BT, TOPK]),
                                ALU.subtract).then_inc(wdiff, 1)
                L(v.tensor_copy(topf, topi[:, :, 0:TOPK]))
                L(v.tensor_tensor(oh[:, :, :, :], K[:, C_IOTA:C_IOTA + E].unsqueeze(1).unsqueeze(1).to_broadcast(JK),
                                  topf.unsqueeze(3).to_broadcast(JK), ALU.is_equal))
                with nc.allow_low_precision("counts up to four are exact in bfloat16"):
                    v.tensor_reduce(chosen[:, :, :], oh[:, :, :, :].rearrange("p j k e -> p j e k"), AX,
                                    ALU.add).then_inc(chosen_ready, 1)

            def row_tails(t, par):
                def product(src):
                    return L.send(v.tensor_tensor(prod[:, :, :, :], oh[:, :, :, :], src.unsqueeze(3).to_broadcast(JK),
                                                  ALU.mult))

                def total(o):
                    return L.send(v.tensor_reduce(o, prod[:, :, :, :].rearrange("p j k e -> p j e k"), AX, ALU.add))

                Wb = Wd[:, ds(BT * t, BT), :]
                n = product(dest)
                dve.wait_ge(wexp_ready, t + 1)
                m = L.send(v.tensor_reduce(wsum, wexp, AX, ALU.add))
                yield
                L.wait(m)
                total(rows[par][:, :, DIM:DIM + E])
                m = L.send(v.reciprocal(wsum, wsum))
                yield
                L.wait(m)
                L.send(v.tensor_scalar(dest, dest, float(TOPK * BLK), None, ALU.add))
                n = L.send(v.tensor_tensor(wexp, wexp, wsum.unsqueeze(2).to_broadcast([P, BT, TOPK]), ALU.mult))
                yield
                L.wait(n)
                n = product(wexp)
                yield
                L.wait(n)
                n = total(Wb)
                yield
                L.wait(n)
                n = L.send(v.tensor_scalar(rows[par][:, :, DIM + E:ROW], Wb, 0.5, None, ALU.mult))
                yield
                L.wait(n)

            def slots(t, par):
                dve.wait_ge(rank_mm, t + 1)
                L(v.tensor_tensor(slot_e[:, :, :], PS[:, 7, 256:256 + BT * E].rearrange("p (j e) -> p j e", e=E),
                                  K[:, C_BASE:C_BASE + E].unsqueeze(1).to_broadcast([P, BT, E]), ALU.add))
                L(v.tensor_tensor(prod[:, :, :, :], oh[:, :, :, :],
                                  slot_e[:, :, :].unsqueeze(2).to_broadcast(JK), ALU.mult))
                L(v.tensor_reduce(slotf, prod[:, :, :, :], AX, ALU.add))
                v.tensor_copy(slot[par].rearrange("p (j k) -> p j k", k=TOPK), slotf).then_inc(slot_ready, 1)
                L(v.tensor_reduce(mstep[:, :], chosen[:, :, :].rearrange("p j e -> p e j"), AX, ALU.add))
                v.tensor_tensor(before[:, :], before[:, :], mstep[:, :], ALU.add).then_inc(before_ready, 1)

            def alternate(one, other):
                chains = [one, other]
                while chains:
                    for chain in list(chains):
                        if next(chain, "end") == "end":
                            chains.remove(chain)

            def step(s, s0, i=None):
                mid, old = on(s0, 1), on(s0, 2)
                pm, po = (s0 - 1) % 2, s0 % 2
                if mid:
                    scan(s - 1, pm)
                if old:
                    residual(s - 2)
                if mid or old:
                    block_norms(s - 1, mid, old)
                if mid:
                    scale_cell(s - 1, pm)
                    hidden(s - 1, pm)
                if old:
                    choose(s - 2, po)
                if mid:
                    y_stats(s - 1)
                alternate(y_norm() if mid else iter(()), row_tails(s - 2, po) if old else iter(()))
                if old:
                    slots(s - 2, po)

            steps(dve, step, L, PER_TURN)

            dve.wait_ge(cnt_mm, 1)
            L(v.tensor_tensor(tab_pad[:, :], PS[0:1, 0, 0:E], K[0:1, C_BASE:C_BASE + E], ALU.add))
            L(v.tensor_scalar(cnt_i, PS[0:E, 1, 0:1], float(P - 1), None, ALU.add))
            L(v.tensor_scalar(cnt_i, cnt_i, 7, None, ALU.logical_shift_right))
            L(v.tensor_copy(nt_col, cnt_i))
            v.tensor_scalar(dl_col, nt_col, -float(P), float(REGION), ALU.mult, ALU.add).then_inc(nt_ready, 1)
            dve.wait_ge(end_mm, 1)
            L(v.tensor_copy(end_col, PS[0:E, 2, 0:1]))
            v.tensor_scalar(ended[:, :], K[0:E, C_TILE:C_TILE + TILES], end_col, None, ALU.is_ge).then_inc(cmp_ready, 1)
            dve.wait_ge(tab_mm, 1)
            L(v.scalar_tensor_tensor(rowf[:, 0, :], K[0:1, C_TILE:C_TILE + TILES], float(P), PS[0:1, 4, 0:TILES],
                                     ALU.mult, ALU.add))
            L(v.tensor_scalar(tab_row[:, :], rowf[:, 0, :], float(PAD0), None, ALU.min))
            v.tensor_scalar(tab_e[:, :], PS[0:1, 3, 0:TILES], float(E - 1), None, ALU.min).then_inc(tab_ready, 1)

            rest = cell[0][:, 0, :]
            mid_part = cell[0][:, 1, 0:FF].bitcast(bf16)
            dve.wait_ge(bias_in, 48)
            L(v.tensor_copy(bias_gu[:, :], bias_src[:, :]))
            L(v.tensor_tensor(rest, bias_src[:, :], bias_gu[:, :], ALU.subtract))
            L(v.tensor_copy(bias_gu[32:64, :], rest[32:64, :]))
            L(v.tensor_copy(mid_part, rest))
            L(v.tensor_tensor(rest, rest, mid_part, ALU.subtract))
            v.tensor_copy(bias_gu[64:96, :], rest[64:96, :]).then_inc(bias_done, 1)

            def tile(j, u):
                b = u % 2
                acc = PS[:, 2 + b, :]
                dve.wait_ge(gu_mm, j + 1)
                v.tensor_scalar(gate[b], acc[:, 0:FF], LIMIT, None, ALU.min).then_inc(gate_ready, 1)
                L(v.tensor_scalar(up[b], acc[:, FF:2 * FF], LIMIT, -LIMIT, ALU.min, ALU.max))
                dve.wait_ge(sg_ready, j + 1)
                L(v.scalar_tensor_tensor(glu[b], sg[b], 1.0, gate[b], ALU.add, ALU.mult))
                v.scalar_tensor_tensor(act_[b], up[b], 1.0, glu[b], ALU.add, ALU.mult).then_inc(act_ready, 1)

            with dve.Fori(0, TURNS) as i:
                L.start(i, 2 * UN)
                for u in range(UN):
                    tile(UN * i + u, u)
            L.stop(TURNS)

            def sum_pairs(g, h):
                dve.wait_ge(zs_ready, BT * g + (2 * h + 2))
                dve.nop(nofuse=True)
                dve.wait_ge(zz_free, 2 * g + (h + 1))
                n = L.send(v.tensor_tensor(zz[h], zs[h][:, :, 0, :], zs[h][:, :, 1, :], ALU.add))
                L.wait(n)
                dve.sem_inc(zs_free, 1)
                dve.sem_inc(zz_ready, 1)

            def add_z(g, b):
                Xb = X[:, ds(BT * g, BT), :]
                dve.wait_ge(yz_ready, g + 3)
                v.tensor_tensor(Xb, Xb, yz[b], ALU.add).then_inc(yo_ready, 1)

            def group(g, b, first=False, last=False):
                def rest():
                    if not last:
                        for h in range(2):
                            sum_pairs(g + 1, h)
                            yield
                    if not first:
                        add_z(g - 1, 1 - b)

                dve.wait_ge(zz_free, 2 * g + 4)
                stats(lambda j: PS[:, 2 + 2 * b + j // 2, (j % 2) * DIM:(j % 2 + 1) * DIM], mv2, LN_EPS)
                alternate(y_norm(rz_ready), rest())

            for h in range(2):
                sum_pairs(0, h)
            group(0, 0, first=True)
            with dve.Fori(0, NBLK // 2 - 1) as i:
                L.start(i, 32)
                group(2 * i + 1, 1)
                group(2 * i + 2, 0)
            L.stop(NBLK // 2 - 1)
            group(NBLK - 1, 1, last=True)
            add_z(NBLK - 1, 1)


def kernel(**inputs):
    import concourse.bacc as bacc
    from concourse.bass_utils import run_bass_kernel_spmd

    a = {n: np.asarray(inputs[n]) for n in inputs}

    def tiles_of(w):
        return np.ascontiguousarray(w.reshape(-1, P, w.shape[-1]).transpose(1, 0, 2))

    order = (3, 0, 1, 2)
    wg = a["L0_attn_W_gate"].reshape(PAIRS, 2, 4, HD, DIM)[:, :, order].transpose(2, 0, 1, 3, 4).reshape(GATES, DIM)
    bg = a["L0_attn_b_gate"].reshape(PAIRS, 2, 4, HD)[:, :, order].transpose(2, 0, 1, 3).reshape(CHUNKS, P)
    gu = a["L0_ffn_gate_up_proj"].reshape(E, KT, P, FF, 2).transpose(2, 0, 1, 4, 3)
    dn = a["L0_ffn_down_proj"].reshape(E, KT, P, DIM).transpose(2, 0, 1, 3)
    cst, cstb = constants()
    arrays = {
        "x": np.ascontiguousarray(a["L0_attn_x"].reshape(TOKENS, DIM)),
        "w_in": tiles_of(a["L0_attn_W_in"]),
        "w_gate": tiles_of(wg.T),
        "b_gate": np.ascontiguousarray(bg.T),
        "rms_w": np.ascontiguousarray(np.tile(a["L0_attn_rms_w"], 2).reshape(P, 1)),
        "w_out": tiles_of(a["L0_attn_W_out"].T),
        "w_router": tiles_of(a["L0_ffn_router_weight"].T),
        "b_router": np.ascontiguousarray(np.broadcast_to(a["L0_ffn_router_bias"], (P, E))),
        "w_gu": np.ascontiguousarray(gu).reshape(P, -1),
        "b_gu": np.ascontiguousarray(a["L0_ffn_gate_up_proj_bias"].reshape(E, FF, 2).transpose(0, 2, 1)).reshape(E, 2 * FF),
        "w_dn": np.ascontiguousarray(dn).reshape(P, -1),
        "b_dn": np.ascontiguousarray(a["L0_ffn_down_proj_bias"]),
        "cst": cst,
        "cstb": cstb,
    }
    nc = bacc.Bacc("TRN2", target_bir_lowering=False, num_devices=1)
    f32 = mybir.dt.float32
    args = [nc.dram_tensor(n, v.shape, f32, kind="ExternalInput").ap() for n, v in arrays.items()]
    out = nc.dram_tensor("out", [TOKENS, DIM], f32, kind="ExternalOutput").ap()
    build(nc, *args, out)
    r = run_bass_kernel_spmd(nc, [arrays], core_ids=[0])
    return r.results[0]["out"].reshape(BATCH, SEQ, DIM)
```

```python
import concourse.bass as bass
from concourse import mybir
from contextlib import ExitStack
import numpy as np

P = 128
BATCH, SEQ, DIM = 16, 256, 256
TOKENS = BATCH * SEQ
HEADS, HD = 4, 64
PAIRS = 2
KT = DIM // P
BLK = 512
BT = BLK // P
NBLK = TOKENS // BLK
NTILE = TOKENS // P
GATES = 4 * DIM
CHUNKS = GATES // P
E, TOPK, FF = 16, 4, 256
ROW = DIM + 2 * E
REGION = TOKENS + P
PAD0 = E * REGION
ZROWS = TOKENS * TOPK
TILES = -(-(ZROWS + E * (P - 1)) // P)
UN = 6
TURNS = -(-TILES // UN)
TILES = TURNS * UN
LIMIT, ALPHA = 7.0, 1.702
LN_EPS, RMS_EPS = 1e-5, 1e-6
MAGIC = float(0x5F3759DF)
ZIN = 8
PART = 1024
PARTS_GU, PARTS_DN = E * KT * 2 * FF // PART, E * KT * DIM // PART
PARTS = PARTS_GU + PARTS_DN
LATE = 6
AHEAD = 3
EARLY_SPLIT = 8
X_BITS, A_BITS = 11, 9
PER_TURN = 96

C_IDENT, C_HALF, C_IOTA, C_BASE, C_DEST, C_SEL = 0, 128, 130, 146, 162, 178
C_TILE = C_SEL + 8 * P
C_TRI16 = C_TILE + TILES
C_PAD = C_TRI16 + E
C_DUMP = C_PAD + ROW
C_LEN = C_DUMP + UN
B_TRI, B_ONE, B_PICK = 0, 128, 256
B_LEN = B_PICK + E * P


def constants():
    c = np.zeros((P, C_LEN), np.float32)
    p = np.arange(P)
    c[:, C_IDENT:C_IDENT + P] = np.eye(P)
    c[:, C_HALF:C_HALF + 2] = (p[:, None] // HD) == np.arange(2)
    c[:, C_IOTA:C_IOTA + E] = np.arange(E)
    c[:, C_BASE:C_BASE + E] = np.arange(E) * REGION
    c[:, C_DEST:C_DEST + BT * TOPK] = (TOPK * (P * np.arange(BT)[None, :, None] + p[:, None, None])
                                       + np.arange(TOPK)).reshape(P, -1)
    for j in range(BT):
        for q in range(PAIRS):
            for half in range(2):
                lo = C_SEL + (j * PAIRS + q) * P + half * HD
                c[j * HEADS + 2 * q + half, lo:lo + HD] = 1.0
    c[:, C_TILE:C_TILE + TILES] = np.arange(TILES)
    c[:E, C_TRI16:C_TRI16 + E] = np.arange(E)[:, None] <= np.arange(E)
    c[:, C_PAD + DIM:C_PAD + DIM + E] = 2 * ZROWS
    c[:, C_DUMP:C_DUMP + UN] = ZROWS + P * np.arange(UN) + p[:, None]
    b = np.zeros((P, B_LEN), np.float32)
    b[:, B_TRI:B_TRI + P] = p[:, None] < p
    b[:, B_ONE:B_ONE + P] = 1.0
    for e in range(E):
        for part in range(3):
            b[32 * part + e, B_PICK + e * P:B_PICK + (e + 1) * P] = 1.0
    return c, b


class Link:

    def __init__(self, eng, sem):
        self.eng, self.sem, self.n, self.turn = eng, sem, 0, 0

    def __call__(self, ins, apart=False):
        ins.then_inc(self.sem, 1)
        self.n += 1
        self.eng.wait_ge(self.sem, self.n + self.turn)
        if apart:
            self.eng.nop(nofuse=True)

    def send(self, ins):
        ins.then_inc(self.sem, 1)
        self.n += 1
        return self.n + self.turn

    def wait(self, count):
        self.eng.wait_ge(self.sem, count)

    def start(self, i, per):
        self.turn, self.per, self.first = i * per, per, self.n

    def stop(self, turns):
        assert self.n - self.first == self.per, (self.n - self.first, self.per)
        self.n, self.turn = self.first + self.per * turns, 0


def build(nc, x, w_in, w_gate, b_gate, rms_w, w_out, w_router, b_router, w_gu, b_gu, w_dn, b_dn,
          cst, cstb, out):
    f32, bf16, f16 = mybir.dt.float32, mybir.dt.bfloat16, mybir.dt.float16
    i32, u32 = mybir.dt.int32, mybir.dt.uint32
    ALU = mybir.AluOpType
    ACT = mybir.ActivationFunctionType
    AX = mybir.AxisListType.X
    ds = bass.ds

    ctx = ExitStack()
    with ctx:
        def sb(name, shape, dt=f32):
            return ctx.enter_context(nc.sbuf_tensor(name, shape, dt))

        def sem(name):
            return ctx.enter_context(nc.semaphore(name))

        routed = nc.dram_tensor("routed", [PAD0 + P, ROW], f32, kind="Internal").ap()
        expert_out = nc.dram_tensor("expert_out", [ZROWS + UN * P, DIM], f32, kind="Internal").ap()

        X = sb("X", [P, NTILE, DIM])
        W = sb("W", [P, (PARTS + AHEAD) * PART])
        K = sb("K", [P, C_LEN])
        KB = sb("KB", [P, B_LEN], bf16)
        Wd = sb("Wd", [P, NTILE, E])
        bias_gu = sb("bias_gu", [P, 2 * FF], bf16)
        Bdn = sb("Bdn", [E, DIM])
        tab_row = sb("tab_row", [1, TILES], i32)
        tab_e = sb("tab_e", [1, TILES], i32)
        tab_pad = sb("tab_pad", [1, E], i32)
        small = sb("small", [P, 1024])
        arena = sb("arena", [P, 11552])
        PS = ctx.enter_context(nc.psum_tensor("PS", [P, 8, 512], f32))

        W16 = W[:, :].bitcast(f16)
        KBf = W[:, 0:B_LEN]
        ident = K[:, C_IDENT:C_IDENT + P]
        triB, oneB = KB[:, B_TRI:B_TRI + P], KB[:, B_ONE:B_ONE + P]

        at = [0]

        def cut(n, parts=P):
            lo = at[0]
            at[0] += n
            assert at[0] <= 11552
            return arena[0:parts, lo:lo + n]

        WcT = cut(KT * GATES).rearrange("p (k g) -> p k g", k=KT)
        WoT = cut(PAIRS * DIM).rearrange("p (k g) -> p k g", k=PAIRS)
        WrT = cut(KT * E).rearrange("p (k g) -> p k g", k=KT)
        xn = cut(BT * DIM).rearrange("p (j d) -> p j d", j=BT)
        xT = cut(KT * BLK).rearrange("p (k t) -> p k t", k=KT)
        stage = at[0]
        g_o = [cut(PAIRS * BLK).rearrange("p (k t) -> p k t", k=PAIRS) for _ in range(2)]
        cell = [cut(PAIRS * BLK).rearrange("p (k t) -> p k t", k=PAIRS) for _ in range(2)]
        WgT = arena[:, stage:stage + KT * GATES].rearrange("p (k g) -> p k g", k=KT)
        WiT = arena[:, stage + KT * GATES:stage + KT * GATES + KT * DIM].rearrange("p (k g) -> p k g", k=KT)
        g_i, g_c, csq, g_f, cn, hT, yn, x2T = [
            W[:, n * PART:(n + 1) * PART].rearrange("p (k t) -> p k t", k=k)
            for n, k in zip((0, 1, *range(PARTS + AHEAD - LATE, PARTS + AHEAD)), (PAIRS,) * 6 + (BT, KT))]
        bias_src = arena[:, stage - KT * BLK - BT * DIM:stage - KT * BLK - BT * DIM + 2 * FF]
        spread = [arena[:, stage - KT * BLK - BT * DIM + 2 * FF + n * P:
                        stage - KT * BLK - BT * DIM + 2 * FF + (n + 1) * P] for n in range(2)]
        bias_rest = arena[:, stage + 2 * PART:stage + 3 * PART]
        junk = cut(PART // 2).bitcast(bf16)
        rows = [cut(BT * ROW).rearrange("p (j d) -> p j d", j=BT) for _ in range(2)]
        at[0] = 0
        xg = [cut(ROW) for _ in range(UN)]
        xh, xl, ah, al = [[cut(DIM // 2).bitcast(f16).rearrange("p (k t) -> p k t", k=KT) for _ in range(2)]
                          for _ in range(4)]
        gate = [cut(FF) for _ in range(2)]
        up = [cut(FF) for _ in range(2)]
        sg = [cut(FF) for _ in range(2)]
        glu = [cut(FF) for _ in range(2)]
        act_ = [cut(FF) for _ in range(2)]
        yb = [cut(DIM) for _ in range(UN)]
        dst = [cut(1).bitcast(u32) for _ in range(UN)]
        dstf = [cut(1) for _ in range(UN)]
        wgt = [cut(1) for _ in range(UN)]
        wraw = [cut(1) for _ in range(UN)]
        zz = [cut(2 * DIM).rearrange("p (u d) -> p u d", u=2) for _ in range(2)]
        sT = [cut(BT * P, E) for _ in range(2)]
        ws = [cut(BT * E).rearrange("p (j e) -> p j e", j=BT) for _ in range(2)]
        yz = [cut(BT * DIM).rearrange("p (j d) -> p j d", j=BT) for _ in range(2)]
        zin = [W[:, n * PART:(n + 1) * PART].rearrange("p (k d) -> p k d", k=TOPK) for n in range(ZIN)]
        zs = [W[:, n * PART:(n + 1) * PART].rearrange("p (u k d) -> p u k d", u=2, k=2)
              for n in range(ZIN, ZIN + ZIN // 2)]

        sat = [0]

        def tiny(n, dt=f32, parts=P):
            lo = sat[0]
            sat[0] += n
            assert sat[0] <= 1024
            v = small[0:parts, lo:lo + n]
            return v if dt == f32 else v.bitcast(dt)

        bG = tiny(CHUNKS)
        rmsw = tiny(1)
        bR = tiny(E)
        mv1 = tiny(NTILE * 2).rearrange("p (j s) -> p j s", s=2)
        r1 = tiny(NTILE)
        nv, na, nb_, ny = tiny(NTILE), tiny(NTILE), tiny(NTILE), tiny(NTILE)
        st2 = tiny(BT * 6).rearrange("p (j s) -> p j s", s=6)
        mv2 = tiny(BT * 2).rearrange("p (j s) -> p j s", s=2)
        mv3 = tiny(BT * 2).rearrange("p (j s) -> p j s", s=2)
        mr1 = tiny(NTILE)
        rs = tiny(BT + BT * HEADS)
        r2, mr2, mr3 = tiny(BT), tiny(BT), tiny(BT)
        rT = tiny(P, parts=BT * HEADS)
        top = tiny(BT * 8).rearrange("p (j s) -> p j s", s=8)
        topi = tiny(BT * 8, u32).rearrange("p (j s) -> p j s", s=8)
        logit = tiny(BT * E).rearrange("p (j s) -> p j s", s=E)
        topf = tiny(BT * TOPK).rearrange("p (j s) -> p j s", s=TOPK)
        wexp = tiny(BT * TOPK).rearrange("p (j s) -> p j s", s=TOPK)
        wsum = tiny(BT)
        dest = tiny(BT * TOPK).rearrange("p (j s) -> p j s", s=TOPK)
        slotf = tiny(BT * TOPK).rearrange("p (j s) -> p j s", s=TOPK)
        slot = [tiny(BT * TOPK, i32) for _ in range(2)]
        nt_col, dl_col, end_col = [tiny(1, parts=E) for _ in range(3)]
        cnt_i = tiny(1, i32, parts=E)
        ssq = tiny(PARTS)
        peak, peak_all, expo = tiny(1), tiny(1), tiny(1, i32)
        w_scale = [tiny(1), tiny(1)]
        gu_one, gu_inv, act_scale, y_inv = tiny(1), tiny(1), tiny(1), tiny(1)
        gu_hi, gu_lo = tiny(1), tiny(1)
        oh = sb("oh", [P, BT, TOPK, E])
        prod = sb("prod", [P, BT, TOPK, E])
        slot_e = sb("slot_e", [P, BT, E])
        chosen = sb("chosen", [P, BT, E], bf16)
        before = sb("before", [P, E], bf16)
        mstep = sb("mstep", [P, E])
        ended = xT[0:E, 0, 0:TILES]
        rowf = xT[0:1, 1, 0:TILES]

        s_const, s_w, s_moe, s_gate = sem("s_const"), sem("s_w"), sem("s_moe"), sem("s_gate")
        s_last = sem("s_last")
        s_late, squared, peak_ready, peak_mm = sem("s_late"), sem("squared"), sem("peak_ready"), sem("peak_mm")
        scale_ready, high_done, low_done = sem("scale_ready"), sem("high_done"), sem("low_done")
        s_x = [sem(f"s_x{b}") for b in range(2)]
        bias_zero, bias_in, bias_done = sem("bias_zero"), sem("bias_in"), sem("bias_done")
        wc_mm, wc_copy, half_b, kb_ready = sem("wc_mm"), sem("wc_copy"), sem("half_b"), sem("kb_ready")
        xn_ready, xT_mm, xT_ready = sem("xn_ready"), sem("xT_mm"), sem("xT_ready")
        gate_mm, gate_act, f_ready = sem("gate_mm"), sem("gate_act"), sem("f_ready")
        u_ready = sem("u_ready")
        cell_ready, csq_ready, ms_mm = sem("cell_ready"), sem("csq_ready"), sem("ms_mm")
        rms_ready, rT_mm, rT_ready, rb_mm = sem("rms_ready"), sem("rT_mm"), sem("rT_ready"), sem("rb_mm")
        cn_ready, tanh_ready, h_ready = sem("cn_ready"), sem("tanh_ready"), sem("h_ready")
        y_mm, r2_ready, yn_ready = sem("y_mm"), sem("r2_ready"), sem("yn_ready")
        r1_ready, r3_ready = sem("r1_ready"), sem("r3_ready")
        x2_ready, x2T_mm, x2T_ready = sem("x2_ready"), sem("x2T_mm"), sem("x2T_ready")
        log_mm, wdiff, wexp_ready = sem("log_mm"), sem("wdiff"), sem("wexp_ready")
        chosen_ready, rank_mm, before_ready = sem("chosen_ready"), sem("rank_mm"), sem("before_ready")
        slot_ready = sem("slot_ready")
        rows_sent = [sem(f"rows_sent{b}") for b in range(2)]
        rows_free = sem("rows_free")
        v_link = sem("v_link")
        cnt_mm, nt_ready, end_mm, cmp_ready = sem("cnt_mm"), sem("nt_ready"), sem("end_mm"), sem("cmp_ready")
        tab_mm, tab_ready, pad_sent = sem("tab_mm"), sem("tab_ready"), sem("pad_sent")
        xg_in = [sem(f"xg_in{u}") for u in range(UN)]
        tr_mm, xh_ready, xl_ready, gu_mm = sem("tr_mm"), sem("xh_ready"), sem("xl_ready"), sem("gu_mm")
        gate_ready, sg_ready, act_ready = sem("gate_ready"), sem("sg_ready"), sem("act_ready")
        aT_mm, ah_ready, al_ready, y2_mm = sem("aT_mm"), sem("ah_ready"), sem("al_ready"), sem("y2_mm")
        y2_ready = sem("y2_ready")
        dst_copied, dst_ready = sem("dst_copied"), sem("dst_ready")
        y_sent = [sem(f"y_sent{u}") for u in range(UN)]
        z_in = [sem(f"z_in{u}") for u in range(ZIN)]
        zs_ready = sem("zs_ready")
        zz_ready, zz_free = sem("zz_ready"), sem("zz_free")
        sT_mm, sT_ready = sem("sT_mm"), sem("sT_ready")
        rz_ready, yz_ready, yo_ready = sem("rz_ready"), sem("yz_ready"), sem("yo_ready")
        out_sent, ws_ready = sem("out_sent"), sem("ws_ready")

        block = ctx.enter_context(nc.Block())
        x_v = x.rearrange("(n p) d -> p n d", p=P)
        out_v = out.rearrange("(n p) d -> p n d", p=P)

        def steps(eng, step, link=None, per=0):
            for s in range(3):
                step(s, s)
            turns = (NBLK - 4) // 2
            with eng.Fori(0, turns) as i:
                if link:
                    link.start(i, per)
                step(2 * i + 3, 3, i)
                step(2 * i + 4, 4, i)
            if link:
                link.stop(turns)
            for s in range(3 + 2 * turns, NBLK + 2):
                step(s, s)

        def experts(eng, first, n):
            _, values = nc.values_load_multi_w_load_instructions(
                tab_e[0:1, ds(first, n)], engines=[eng], min_val=0, max_val=E - 1,
                skip_runtime_bounds_check_because="the table holds counts, capped at the last expert")
            return values

        def tiles(eng, step, link=None, per=0, name=None):
            def run(first, lo, hi, at, i=None):
                known = experts(name, at, min(hi, TILES) - first) if name else None
                for uj in range(lo, hi):
                    j = uj if i is None else UN * i + uj
                    if name:
                        step(j, uj, i, known[uj - first] if uj - first < len(known) else None,
                             known[uj - 3 - first] if uj - 3 >= first else None)
                    else:
                        step(j, uj, i)

            run(0, 0, UN + 2, 0)
            with eng.Fori(0, TURNS - 2) as i:
                if link:
                    link.start(i, per)
                run(UN - 1, UN + 2, 2 * UN + 2, UN * i + (UN - 1), i)
            if link:
                link.stop(TURNS - 2)
            run(TILES - UN - 1, TILES - UN + 2, TILES + 3, TILES - UN - 1)

        def source(c):
            return W[:, ds((c + AHEAD) * PART, PART)]

        def halves(c, down):
            both = W16[:, ds(c * (2 * PART), 2 * PART)].rearrange("p (e h x) -> p h e x", e=2 if down else 1, h=2)
            return both[:, 0, :, :], both[:, 1, :, :]

        def on(s0, lag):
            return 0 <= s0 - lag < NBLK

        @block.sync
        def _(sp):
            sp.sem_inc(rows_free, 2)
            sp.sem_inc(low_done, AHEAD)
            sp.sem_inc(squared, 1)
            sp.sem_inc(zz_free, ZIN // 2)
            sp.sem_inc(y2_ready, 2)
            sp.sem_inc(yz_ready, 2)
            def load_x(b):
                sp.dma_start(X[:, BT * b:BT * (b + 1), :], x_v[:, BT * b:BT * (b + 1), :]).then_inc(s_x[b % 2], 16)

            sp.dma_start(WiT, w_in).then_inc(s_gate, 16)
            sp.dma_start(WgT, w_gate).then_inc(s_gate, 16)
            load_x(0)
            sp.dma_start(K[:, :], cst).then_inc(s_const, 16)
            load_x(1)
            sp.dma_start(KBf, cstb).then_inc(s_const, 16)
            sp.dma_start(WoT, w_out).then_inc(s_w, 16)
            sp.dma_start(WrT, w_router).then_inc(s_w, 16)
            sp.dma_start(bG, b_gate).then_inc(s_w, 16)
            sp.dma_start(rmsw, rms_w).then_inc(s_w, 16)
            sp.dma_start(bR, b_router).then_inc(s_w, 16)
            for b in range(2, NBLK):
                sp.wait_ge(s_x[b % 2], 16 * (b // 2))
                load_x(b)
            sp.dma_start(Bdn[:, :], b_dn).then_inc(s_moe, 16)
            sp.wait_ge(kb_ready, 1)

            def load_weights(lo, hi, done):
                w, first = (w_gu, 0) if lo < PARTS_GU else (w_dn, PARTS_GU)
                sp.dma_start(W[:, (lo + AHEAD) * PART:(hi + AHEAD) * PART],
                             w[:, (lo - first) * PART:(hi - first) * PART]).then_inc(done, 16)

            for c in range(0, PARTS - LATE, 2):
                load_weights(c, c + 2, s_moe)
            sp.wait_ge(bias_zero, 1)
            for part in range(3):
                sp.dma_start(bias_src[32 * part:32 * part + E, :], b_gu).then_inc(bias_in, 16)
            sp.wait_ge(y_mm, NBLK)
            for c in range(PARTS - LATE, PARTS - 2, 2):
                load_weights(c, c + 2, s_late)
            sp.wait_ge(log_mm, NBLK)
            load_weights(PARTS - 2, PARTS, s_last)

            sp.wait_ge(tab_ready, 1)
            pad = K[:, C_PAD:C_PAD + ROW]
            for e in range(E):
                first = sp.value_load(tab_pad[0:1, e:e + 1], min_val=e * REGION, max_val=e * REGION + TOKENS)
                sp.dma_start(routed[ds(first, P), :], pad).then_inc(pad_sent, 16)
            sp.dma_start(routed[PAD0:PAD0 + P, :], pad).then_inc(pad_sent, 16)
            sp.wait_ge(pad_sent, 16 * (E + 1))
            for b in range(2):
                sp.wait_ge(rows_sent[b], 16 * BT * TOPK * NBLK // 2)

            def load_tile(j, u):
                r = sp.value_load(tab_row[0:1, ds(j, 1)], min_val=0, max_val=PAD0)
                sp.dma_start(xg[u], routed[ds(r, P), :]).then_inc(xg_in[u], 16)

            for u in range(UN):
                load_tile(u, u)
            with sp.Fori(1, TURNS) as i:
                for u in range(UN):
                    sp.wait_ge(tr_mm, UN * i + (u + 1 - UN))
                    sp.wait_ge(dst_ready, UN * i + (u + 1 - UN))
                    load_tile(UN * i + u, u)

            for u in range(UN):
                sp.wait_ge(y_sent[u], 16 * TURNS)
            z_v = expert_out[0:ZROWS, :].rearrange("(n p k) d -> n p k d", p=P, k=TOPK)

            def load_z(n, u):
                sp.dma_start(zin[u], z_v[ds(n, 1), :, :, :].rearrange("n p k d -> (n p) k d")).then_inc(z_in[u], 16)

            for u in range(ZIN):
                load_z(u, u)
            with sp.Fori(1, NTILE // ZIN) as i:
                for u in range(ZIN):
                    sp.wait_ge(zs_ready, ZIN * i + (u + 1 - ZIN))
                    load_z(ZIN * i + u, u)
            sp.wait_ge(out_sent, 16 * NBLK)

        @block.tensor
        def _(pe):
            mm = nc.tensor.matmul

            pe.wait_ge(s_gate, 16 * 2)
            for n in range(2):
                for m in range(KT):
                    for k in range(KT):
                        last = mm(PS[:, 2 * n + m, :], WiT[:, k, m * P:(m + 1) * P],
                                  WgT[:, k, n * 512:(n + 1) * 512], start=(k == 0), stop=(k == KT - 1))
                    last.then_inc(wc_mm, 1)

            def transposes_x(t):
                pe.wait_ge(xn_ready, t + 1)
                for k in range(KT):
                    for j in range(BT):
                        last = nc.tensor.transpose(PS[:, k, j * P:(j + 1) * P], xn[:, j, k * P:(k + 1) * P], ident)
                    last.then_inc(xT_mm, 1)

            def gates(t, c, first):
                if first or c >= 2:
                    pe.wait_ge(gate_act, 8 * t + (c - 1))
                for k in range(KT):
                    if c == 0:
                        pe.wait_ge(xT_ready, 2 * t + (k + 1))
                    last = mm(PS[:, 2 + c % 2, :], WcT[:, k, c * P:(c + 1) * P], xT[:, k, :],
                              start=(k == 0), stop=(k == KT - 1))
                last.then_inc(gate_mm, 1)

            def mean_square(t):
                pe.wait_ge(csq_ready, t + 1)
                for j in range(BT):
                    for q in range(PAIRS):
                        last = mm(PS[:, 6, HEADS * j + 2 * q:HEADS * j + 2 * q + 2], csq[:, q, j * P:(j + 1) * P],
                                  K[:, C_HALF:C_HALF + 2], start=True, stop=True)
                last.then_inc(ms_mm, 1)

            def rms_transpose(t):
                pe.wait_ge(rms_ready, t + 1)
                nc.tensor.transpose(PS[0:BT * HEADS, 6, P:2 * P], rs[:, BT:BT + BT * HEADS], ident).then_inc(rT_mm, 1)

            def rms_spread(t, later):
                pe.wait_ge(rT_ready, t + 1)
                if later:
                    pe.wait_ge(yn_ready, t)
                for q in range(PAIRS):
                    for j in range(BT):
                        lo = C_SEL + (j * PAIRS + q) * P
                        last = mm(PS[:, 4 + q, j * P:(j + 1) * P], K[0:BT * HEADS, lo:lo + P], rT,
                                  start=True, stop=True)
                last.then_inc(rb_mm, 1)

            def out_product(t):
                pe.wait_ge(h_ready, t + 1)
                for j in range(BT):
                    for q in range(PAIRS):
                        last = mm(PS[:, 4 + j // 2, (j % 2) * DIM:(j % 2 + 1) * DIM], hT[:, q, j * P:(j + 1) * P],
                                  WoT[:, q, :], start=(q == 0), stop=(q == PAIRS - 1))
                last.then_inc(y_mm, 1)

            def transposes_x2(t, rw):
                pe.wait_ge(x2_ready, t + 1)
                for k in range(KT):
                    for j in range(BT):
                        last = nc.tensor.transpose(PS[:, k, j * P:(j + 1) * P], rw[:, j, k * P:(k + 1) * P], ident)
                    last.then_inc(x2T_mm, 1)

            def logits(t, later):
                if later:
                    pe.wait_ge(slot_ready, t)
                pe.wait_ge(x2T_ready, 2 * t + 2)
                for j in range(BT):
                    for k in range(KT):
                        last = mm(PS[:, 7, E * j:E * (j + 1)], x2T[:, k, j * P:(j + 1) * P], WrT[:, k, :],
                                  start=(k == 0), stop=(k == KT - 1))
                last.then_inc(log_mm, 1)

            def ranks(t):
                pe.wait_ge(chosen_ready, t + 1)
                pe.wait_ge(before_ready, t + 1)
                R = PS[:, 7, 256:256 + BT * E].rearrange("p (j e) -> p j e", e=E)
                mm(R, triB, chosen[:, :, :], start=True, stop=False)
                mm(R, oneB, before[:, :].unsqueeze(1).to_broadcast([P, BT, E]), start=False, stop=False)
                for j in range(BT - 1):
                    last = mm(R[:, j + 1:BT, :], oneB,
                              chosen[:, j:j + 1, :].to_broadcast([P, BT - 1 - j, E]),
                              start=False, stop=(j == BT - 2))
                last.then_inc(rank_mm, 1)

            def peaks(which):
                pe.wait_ge(peak_ready, which + 1)
                nc.tensor.transpose(PS[:, 2, which * P:(which + 1) * P], spread[which], ident).then_inc(peak_mm, 1)

            def step(s, s0, i=None):
                new, mid, old = on(s0, 0), on(s0, 1), on(s0, 2)
                for c in range(CHUNKS):
                    if c == CHUNKS - 1 and on(s0, -1):
                        transposes_x(s + 1)
                    if new:
                        gates(s, c, s0 > 0)
                    if c == 1 and mid:
                        mean_square(s - 1)
                    if c == 3 and mid:
                        rms_transpose(s - 1)
                    if c == 3 and s0 == NBLK:
                        pe.wait_ge(gate_act, 8 * NBLK)
                        peaks(0)
                    if c == 3 and mid:
                        rms_spread(s - 1, s0 > 1)
                    if c == 3 and old:
                        transposes_x2(s - 2, rows[s0 % 2])
                    if c == 4 and old:
                        logits(s - 2, s0 > 2)
                    if c == 4 and mid:
                        out_product(s - 1)
                    if c == 6 and old:
                        ranks(s - 2)

            pe.wait_ge(s_const, 32)
            pe.wait_ge(s_w, 16 * 5)
            pe.wait_ge(wc_copy, 4)
            transposes_x(0)
            pe.wait_ge(kb_ready, 1)
            steps(pe, step)

            pe.wait_ge(before_ready, NBLK + 1)
            mm(PS[0:1, 0, 0:E], KB[:, B_ONE:B_ONE + 1], before[:, :], start=True, stop=True)
            mm(PS[0:E, 1, 0:1], before[:, :], KB[:, B_ONE:B_ONE + 1], start=True, stop=True).then_inc(cnt_mm, 1)
            pe.wait_ge(nt_ready, 1)
            mm(PS[0:E, 2, 0:1], K[0:E, C_TRI16:C_TRI16 + E], nt_col, start=True, stop=True).then_inc(end_mm, 1)
            pe.wait_ge(cmp_ready, 1)
            mm(PS[0:1, 3, 0:TILES], K[0:E, C_TRI16 + E - 1:C_TRI16 + E], ended, start=True, stop=True)
            mm(PS[0:1, 4, 0:TILES], dl_col, ended, start=True, stop=True).then_inc(tab_mm, 1)

            pe.wait_ge(tab_ready, 1)
            peaks(1)
            pe.wait_ge(bias_done, 1)
            pe.wait_ge(low_done, PARTS + AHEAD)

            def tile_transposes(j, uj, i):
                pe.wait_ge(xg_in[uj % UN], 16 * (uj // UN + 1) if i is None else 16 * i + 16 * (uj // UN + 1))
                for k in range(KT):
                    last = nc.tensor.transpose(PS[:, uj % 2, k * P:(k + 1) * P],
                                               xg[uj % UN][:, k * P:(k + 1) * P], ident)
                last.then_inc(tr_mm, 1)

            def gate_up(j, uj, e):
                acc = PS[:, 2 + uj % 2, :]
                mm(acc, KB[:, ds(e * P + B_PICK, P)], bias_gu[:, :], start=True, stop=False)
                pe.wait_ge(xh_ready, j + 1)
                pe.wait_ge(xl_ready, j + 1)
                w = W16[:, ds(e * (2 * PART), 2 * PART)]
                for k in range(KT):
                    hi, lo = [w[:, h * PART + k * 2 * FF:h * PART + (k + 1) * 2 * FF] for h in range(2)]
                    mm(acc, xh[uj % 2][:, k, :], hi, start=False, stop=False)
                    mm(acc, xh[uj % 2][:, k, :], lo, start=False, stop=False)
                    last = mm(acc, xl[uj % 2][:, k, :], hi, start=False, stop=(k == KT - 1))
                last.then_inc(gu_mm, 1)

            def act_transposes(j, uj):
                pe.wait_ge(act_ready, j + 1)
                for k in range(KT):
                    last = nc.tensor.transpose(PS[:, 4 + uj % 2, k * P:(k + 1) * P],
                                               act_[uj % 2][:, k * P:(k + 1) * P], ident)
                last.then_inc(aT_mm, 1)

            def down(j, uj, e):
                pe.wait_ge(y2_ready, j + 1)
                pe.wait_ge(ah_ready, j + 1)
                pe.wait_ge(al_ready, j + 1)
                acc = PS[:, 6 + uj % 2, 0:DIM]
                w = W16[:, ds(e * PART + PARTS_GU * 2 * PART, PART)]
                for k in range(KT):
                    hi, lo = [w[:, h * PART // 2 + k * DIM:h * PART // 2 + (k + 1) * DIM] for h in range(2)]
                    mm(acc, ah[uj % 2][:, k, :], hi, start=(k == 0), stop=False)
                    mm(acc, ah[uj % 2][:, k, :], lo, start=False, stop=False)
                    last = mm(acc, al[uj % 2][:, k, :], hi, start=False, stop=(k == KT - 1))
                last.then_inc(y2_mm, 1)

            def tile_step(j, uj, i, new, old):
                running = i is not None
                if uj == 0:
                    tile_transposes(0, 0, None)
                if running or j + 1 < TILES:
                    tile_transposes(j + 1, uj + 1, i)
                if uj >= 2 and (running or j - 2 < TILES):
                    act_transposes(j - 2, uj - 2)
                if uj >= 3:
                    down(j - 3, uj - 3, old)
                if running or j < TILES:
                    gate_up(j, uj, new)

            tiles(pe, tile_step, name=mybir.EngineType.PE)

            def transpose_weights(g, b):
                pe.wait_ge(ws_ready, g + 1)
                for u in range(BT):
                    last = nc.tensor.transpose(PS[0:E, b, u * P:(u + 1) * P], ws[b][:, u, :], ident)
                last.then_inc(sT_mm, 1)

            def combine(g, b, more=True):
                pe.wait_ge(sT_ready, g + 1)
                pe.wait_ge(yz_ready, g + 1)
                for h in range(2):
                    for u in range(2):
                        mm(PS[:, 2 + 2 * b + h, u * DIM:(u + 1) * DIM], sT[b][:, (2 * h + u) * P:(2 * h + u + 1) * P],
                           Bdn[:, :], start=(u == 0), stop=False)
                if more:
                    transpose_weights(g + 1, 1 - b)
                for h in range(2):
                    pe.wait_ge(zz_ready, 2 * g + (h + 1))
                    mm(PS[:, 2 + 2 * b + h, :], ident, zz[h], start=False, stop=True).then_inc(zz_free, 1)

            transpose_weights(0, 0)
            with pe.Fori(0, NBLK // 2 - 1) as i:
                for b in range(2):
                    combine(2 * i + b, b)
            combine(NBLK - 2, 0)
            combine(NBLK - 1, 1, False)

        @block.scalar
        def _(act):
            def copy(o, i, **kw):
                return nc.scalar.activation(o, i, ACT.Copy, **kw)

            for n in range(2):
                for m in range(KT):
                    act.wait_ge(wc_mm, 2 * n + m + 1)
                    copy(WcT[:, m, n * 512:(n + 1) * 512], PS[:, 2 * n + m, :]).then_inc(wc_copy, 1)

            def evac_x(t):
                for k in range(KT):
                    act.wait_ge(xT_mm, 2 * t + (k + 1))
                    copy(xT[:, k, :], PS[:, k, :]).then_inc(xT_ready, 1)

            def gate_chunk(t, c, s0):
                kind, q = c // 2, c % 2
                if c == 0 and s0 >= 1:
                    act.wait_ge(u_ready, t)
                if c == 2 and s0 >= 1:
                    act.wait_ge(cell_ready, t)
                if c == 6 and s0 >= 2:
                    act.wait_ge(h_ready, t - 1)
                act.wait_ge(gate_mm, 8 * t + (c + 1))
                nc.scalar.activation((g_c, g_i, g_f, g_o[s0 % 2])[kind][:, q, :], PS[:, 2 + c % 2, :],
                                     ACT.Exp if kind == 1 else ACT.Tanh, bias=bG[:, c:c + 1],
                                     scale=1.0 if kind < 2 else 0.5).then_inc(gate_act, 1)
                if c == 5:
                    act.wait_ge(gate_act, 8 * t + 6)
                    copy(g_f, g_f, bias=0.5, scale=0.5).then_inc(f_ready, 1)

            def norm_x(t):
                for j in range(BT):
                    n = ds(BT * t + j, 1)
                    last = nc.scalar.activation(xn[:, j, :], X[:, n, :].rearrange("p n d -> p (n d)"), ACT.Identity,
                                                bias=mr1[:, n], scale=r1[:, n])
                last.then_inc(xn_ready, 1)

            def norm_x1(t, par):
                act.wait_ge(r3_ready, t + 1)
                act.wait_ge(rows_free, t + 1)
                for j in range(BT):
                    last = nc.scalar.activation(rows[par][:, j, 0:DIM],
                                                X[:, ds(BT * t + j, 1), :].rearrange("p n d -> p (n d)"),
                                                ACT.Identity, bias=mr3[:, j:j + 1], scale=rs[:, j:j + 1])
                last.then_inc(x2_ready, 1)

            def square(t, par, later):
                act.wait_ge(cell_ready, t + 1)
                if later:
                    act.wait_ge(ms_mm, t)
                nc.scalar.activation(csq, cell[par], ACT.Square).then_inc(csq_ready, 1)

            def rms_row(t):
                act.wait_ge(rT_mm, t + 1)
                copy(rT, PS[0:BT * HEADS, 6, P:2 * P]).then_inc(rT_ready, 1)

            def tanh_c(t):
                act.wait_ge(cn_ready, t + 1)
                nc.scalar.activation(cn, cn, ACT.Tanh, scale=rmsw).then_inc(tanh_ready, 1)

            def norm_y(t):
                act.wait_ge(r2_ready, t + 1)
                for j in range(BT):
                    last = nc.scalar.activation(yn[:, j, :], PS[:, 4 + j // 2, (j % 2) * DIM:(j % 2 + 1) * DIM],
                                                ACT.Identity, bias=mr2[:, j:j + 1], scale=r2[:, j:j + 1])
                last.then_inc(yn_ready, 1)

            def evac_x2(t):
                for k in range(KT):
                    act.wait_ge(x2T_mm, 2 * t + (k + 1))
                    copy(x2T[:, k, :], PS[:, k, :]).then_inc(x2T_ready, 1)

            def weights_exp(t):
                act.wait_ge(wdiff, t + 1)
                nc.scalar.activation(wexp, wexp, ACT.Exp).then_inc(wexp_ready, 1)

            def squares(c):
                act.wait_ge(squared, c + 1)
                nc.scalar.activation(junk, source(c), ACT.Square, accum_out=ssq[:, ds(c, 1)]).then_inc(squared, 1)

            def high(c, down):
                act.wait_ge(low_done, c + 1)
                hi, lo = halves(c, down)
                nc.scalar.activation(hi, source(c).rearrange("p (e x) -> p e x", e=2 if down else 1), ACT.Copy,
                                     scale=w_scale[down]).then_inc(high_done, 1)

            def step(s, s0, i=None):
                new, mid, old = on(s0, 0), on(s0, 1), on(s0, 2)
                if s0 == NBLK + 1:
                    act.wait_ge(s_late, 16 * (LATE - 2) // 2)
                    for c in range(PARTS - LATE, PARTS - 2):
                        squares(c)
                for c in range(CHUNKS):
                    if c == 4 and old:
                        evac_x2(s - 2)
                    if c == 4 and mid:
                        tanh_c(s - 1)
                    if c == 0 and mid:
                        square(s - 1, (s0 - 1) % 2, s0 > 1)
                    if c == CHUNKS - 1 and s0 == NBLK:
                        act.wait_ge(scale_ready, 1)
                        for part in range(4):
                            high(part, 0)
                    if c == CHUNKS - 1 and mid:
                        norm_y(s - 1)
                    if c == CHUNKS - 1 and on(s0, -1):
                        act.wait_ge(gate_mm, 8 * s + 8)
                        evac_x(s + 1)
                    if new:
                        gate_chunk(s, c, s0)
                    if c == 1 and on(s0, -1):
                        if s0 < 2:
                            act.wait_ge(r1_ready, s0 + 2)
                        norm_x(s + 1)
                    if c == 3 and mid:
                        rms_row(s - 1)
                    if c == 3 and old:
                        norm_x1(s - 2, s0 % 2)
                    if c == 4 and s0 == NBLK + 1:
                        for part in (4, 5):
                            high(part, 0)
                    if c == 5 and old:
                        weights_exp(s - 2)
                    if c == 5 and s0 == NBLK + 1:
                        for part in range(6, EARLY_SPLIT):
                            high(part, 0)
                    if i is not None and c == 4:
                        if s0 == 3:
                            act.wait_ge(s_moe, 16 * (1 + (PARTS - LATE) // 2))
                        for n in range(4):
                            squares(4 * s + (n - 12))
                if s0 == NBLK - 1:
                    for c in range(PARTS_GU, PARTS - LATE):
                        squares(c)

            act.wait_ge(r1_ready, 1)
            norm_x(0)
            evac_x(0)
            act.wait_ge(half_b, 1)
            steps(act, step)

            act.wait_ge(s_last, 16)
            for c in range(PARTS - 2, PARTS):
                squares(c)
            with act.Fori(0, (PARTS_GU - EARLY_SPLIT) // 4) as i:
                for n in range(EARLY_SPLIT, EARLY_SPLIT + 4):
                    high(4 * i + n, 0)
            act.wait_ge(scale_ready, 2)
            with act.Fori(0, PARTS_DN // 4) as i:
                for n in range(PARTS_GU, PARTS_GU + 4):
                    high(4 * i + n, 1)

            def evac_tile(j, uj):
                act.wait_ge(tr_mm, j + 1)
                copy(xh[uj % 2], PS[:, uj % 2, 0:DIM].rearrange("p (k t) -> p k t", k=KT),
                     scale=float(2 ** X_BITS)).then_inc(xh_ready, 1)

            def tile_step(j, uj, i=None):
                running = i is not None
                if uj == 0:
                    evac_tile(0, 0)
                if running or j + 1 < TILES:
                    evac_tile(j + 1, uj + 1)
                if uj >= 1 and (running or j - 1 < TILES):
                    act.wait_ge(gate_ready, j)
                    nc.scalar.activation(sg[(uj + 1) % 2], gate[(uj + 1) % 2], ACT.Tanh, scale=ALPHA / 2).then_inc(sg_ready, 1)
                if uj >= 2 and (running or j - 2 < TILES):
                    act.wait_ge(aT_mm, j - 1)
                    copy(ah[uj % 2], PS[:, 4 + uj % 2, 0:FF].rearrange("p (k t) -> p k t", k=KT),
                         scale=act_scale).then_inc(ah_ready, 1)
                if uj >= 3:
                    u = (uj - 3) % UN
                    act.wait_ge(dst_ready, j - 2)
                    if uj - 3 >= UN:
                        turn = (uj - 3) // UN
                        act.wait_ge(y_sent[u], 16 * i + 16 * turn if running else 16 * turn)
                    act.wait_ge(y2_mm, j - 2)
                    copy(yb[u], PS[:, 6 + (uj + 1) % 2, 0:DIM], scale=wgt[u]).then_inc(y2_ready, 1)
            tiles(act, tile_step)

            def store(g):
                act.wait_ge(yo_ready, g + 1)
                act.dma_start(out_v[:, ds(BT * g, BT), :], X[:, ds(BT * g, BT), :]).then_inc(out_sent, 16)

            def stage_weights(g, b):
                copy(ws[b], Wd[:, ds(BT * g, BT), :]).then_inc(ws_ready, 1)

            def evac_weights(g, b):
                act.wait_ge(sT_mm, g + 1)
                copy(sT[b], PS[0:E, b, :]).then_inc(sT_ready, 1)

            for g in range(2):
                stage_weights(g, g)
            for g in range(NBLK + 2):
                b = g % 2
                if g < NBLK:
                    evac_weights(g, b)
                if g + 2 < NBLK:
                    stage_weights(g + 2, b)
                if g >= 2:
                    act.wait_ge(rz_ready, g - 1)
                    for u in range(BT):
                        last = nc.scalar.activation(
                            yz[b][:, u, :], PS[:, 2 + 2 * b + u // 2, (u % 2) * DIM:(u % 2 + 1) * DIM],
                            ACT.Identity, bias=mr2[:, u:u + 1], scale=r2[:, u:u + 1])
                    last.then_inc(yz_ready, 1)
                if g >= 3:
                    store(g - 3)
            store(NBLK - 1)

        @block.gpsimd
        def _(pool):
            def wait(s, n):
                pool.wait_ge(s, n)
                if not isinstance(n, int):
                    pool.nop(nofuse=True)

            def scatter(t, b, i):
                wait(slot_ready, t + 1)
                for jk in range(BT * TOPK):
                    idx = slot[b][:, jk:jk + 1].bitcast(u32)
                    pool.indirect_dma_start(routed, bass.IndirectOffsetOnAxis(ap=idx, axis=0),
                                            rows[b][:, jk // TOPK, :], None).then_inc(rows_sent[b], 16)
                pool.wait_ge(rows_sent[b], 16 * BT * TOPK * i + 16 * BT * TOPK)
                pool.sem_inc(rows_free, 1)

            with pool.Fori(0, NBLK // 2) as i:
                for b in range(2):
                    scatter(2 * i + b, b, i)

            pool.wait_ge(tab_ready, 1)

            def tile_step(j, uj, i, e, _):
                running = i is not None
                if uj >= 2 and (running or j - 2 < TILES):
                    u = (uj - 2) % UN
                    wait(y2_ready, j + 1)
                    pool.indirect_dma_start(expert_out, bass.IndirectOffsetOnAxis(ap=dst[u], axis=0),
                                            yb[u], None).then_inc(y_sent[u], 16)
                if running or j < TILES:
                    u = uj % UN
                    turn = uj // UN
                    if turn:
                        wait(y_sent[u], 16 * i + 16 * turn if running else 16 * turn)
                    wait(xg_in[u], 16 * i + (16 + 16 * turn) if running else 16 + 16 * turn)
                    pool.tensor_copy(wraw[u], xg[u][:, ds(e + (DIM + E), 1)])
                    pool.tensor_copy(dstf[u], xg[u][:, ds(e + DIM, 1)]).then_inc(dst_copied, 1)
                    wait(dst_copied, j + 1)
                    pool.tensor_scalar(wgt[u], wraw[u], y_inv, None, ALU.mult)
                    pool.tensor_scalar(dst[u], dstf[u], K[:, C_DUMP + u:C_DUMP + u + 1], None,
                                       ALU.min).then_inc(dst_ready, 1)

            pool.wait_ge(scale_ready, 2)
            pool.wait_ge(bias_done, 1)
            tiles(pool, tile_step, name=mybir.EngineType.Pool)

            def pair_sums(n, u, i):
                wait(z_in[u], 16 * i + 16)
                if u % 2 == 0:
                    wait(zz_free, (ZIN // 2) * i + (u // 2 + 1))
                pool.tensor_tensor(zs[u // 2][:, u % 2], zin[u][:, 0:2, :], zin[u][:, 2:4, :], ALU.add).then_inc(zs_ready, 1)

            with pool.Fori(0, NTILE // ZIN) as i:
                for u in range(ZIN):
                    pair_sums(ZIN * i + u, u, i)

        @block.vector
        def _(dve):
            v = nc.vector
            L = Link(dve, v_link)

            def newton(w, o, last=None):
                a, b, y, s = na[:, 0:w], nb_[:, 0:w], ny[:, 0:w], nv[:, 0:w]
                L(v.tensor_scalar(a.bitcast(i32), s.bitcast(i32), 1, None, ALU.logical_shift_right))
                L(v.tensor_scalar(y.bitcast(i32), a.bitcast(i32), -1.0, MAGIC, ALU.mult, ALU.add))
                for n in range(3):
                    L(v.tensor_tensor(a, y, y, ALU.mult))
                    L(v.scalar_tensor_tensor(b, a, -0.5, s, ALU.mult, ALU.mult))
                    (last if last and n == 2 else L)(
                        v.scalar_tensor_tensor(y if n < 2 else o, b, 1.5, y, ALU.add, ALU.mult))

            v.memset(before[:, :], 0.0).then_inc(before_ready, 1)

            def stats_x(place):
                for j in range(BT):
                    last = v.bn_stats(st2[:, j, :], X[:, ds(place + j, 1), :].rearrange("p n d -> p (n d)"))
                L(last, True)
                for j in range(BT):
                    last = v.bn_aggr(mv2[:, j, :], st2[:, j, :])
                L(last)
                L(v.tensor_copy(mv1[:, ds(place, BT), :], mv2))

            def norms_x(lo, hi):
                L(v.tensor_scalar(nv[:, 0:hi - lo], mv1[:, lo:hi, 1], LN_EPS, None, ALU.add))
                newton(hi - lo, r1[:, lo:hi])
                v.scalar_tensor_tensor(mr1[:, lo:hi], mv1[:, lo:hi, 0], -1.0, r1[:, lo:hi], ALU.mult,
                                       ALU.mult).then_inc(r1_ready, 1)

            dve.wait_ge(s_x[0], 16)
            stats_x(0)
            norms_x(0, BT)
            dve.wait_ge(s_w, 16 * 5)
            v.tensor_scalar(bG[:, 4:8], bG[:, 4:8], 0.5, None, ALU.mult).then_inc(half_b, 1)
            dve.wait_ge(s_const, 32)
            v.tensor_copy(KB[:, :], KBf).then_inc(kb_ready, 1)
            L(v.tensor_copy(dest, K[:, C_DEST:C_DEST + BT * TOPK].rearrange("p (j k) -> p j k", k=TOPK)))
            dve.wait_ge(s_x[1], 16)
            stats_x(BT)
            norms_x(BT, 2 * BT)
            with dve.Fori(1, NBLK // 2) as i:
                L.start(i - 1, 6)
                for b in range(2):
                    dve.wait_ge(s_x[b], 16 * i + 16)
                    dve.nop(nofuse=True)
                    stats_x(2 * BT * i + BT * b)
            L.stop(NBLK // 2 - 1)

            def scan(t, par):
                dve.wait_ge(gate_act, 8 * t + 4)
                L(v.tensor_tensor(g_i, g_i, g_c, ALU.mult))
                dve.sem_inc(u_ready, 1)
                dve.wait_ge(f_ready, t + 1)
                for q in range(PAIRS):
                    for b in range(BLK // SEQ):
                        w = slice(b * SEQ, (b + 1) * SEQ)
                        last = v.tensor_tensor_scan(cell[par][:, q, w], g_f[:, q, w], g_i[:, q, w], 0.0,
                                                    ALU.mult, ALU.add)
                last.then_inc(cell_ready, 1)

            def stats(src, mv, eps):
                dve.nop(nofuse=True)
                for j in range(BT):
                    last = v.bn_stats(st2[:, j, :], src(j))
                L(last, True)
                for j in range(BT):
                    last = v.bn_aggr(mv[:, j, :], st2[:, j, :])
                L(last)
                L(v.tensor_scalar(nv[:, 0:BT], mv[:, :, 1], eps, None, ALU.add))

            def residual(t):
                Xb = X[:, ds(BT * t, BT), :]
                dve.wait_ge(yn_ready, t + 1)
                L(v.tensor_tensor(Xb, Xb, yn, ALU.add))
                stats(lambda j: X[:, ds(BT * t + j, 1), :].rearrange("p n d -> p (n d)"), mv3, LN_EPS)

            def block_norms(t, mid, old):
                if not old:
                    L(v.memset(nv[:, 0:BT], 1.0))
                if mid:
                    dve.wait_ge(ms_mm, t + 1)
                    L(v.tensor_scalar(nv[:, BT:BT + BT * HEADS], PS[:, 6, 0:BT * HEADS], 1.0 / HD, RMS_EPS,
                                      ALU.mult, ALU.add))

                    def done(ins):
                        ins.then_inc(rms_ready, 1)
                        dve.wait_ge(rms_ready, t + 1)
                    newton(BT + BT * HEADS, rs, done)
                else:
                    newton(BT, rs[:, 0:BT])
                if old:
                    v.scalar_tensor_tensor(mr3, mv3[:, :, 0], -1.0, rs[:, 0:BT], ALU.mult, ALU.mult).then_inc(r3_ready, 1)

            def y_stats(t):
                dve.wait_ge(y_mm, t + 1)
                stats(lambda j: PS[:, 4 + j // 2, (j % 2) * DIM:(j % 2 + 1) * DIM], mv2, 4 * LN_EPS)

            def y_norm(done=r2_ready):
                a, b, y, x = na[:, 0:BT], nb_[:, 0:BT], ny[:, 0:BT], nv[:, 0:BT]
                n = L.send(v.tensor_scalar(a.bitcast(i32), x.bitcast(i32), 1, None, ALU.logical_shift_right))
                yield
                L.wait(n)
                n = L.send(v.tensor_scalar(y.bitcast(i32), a.bitcast(i32), -1.0, MAGIC, ALU.mult, ALU.add))
                for turn in range(3):
                    yield
                    L.wait(n)
                    n = L.send(v.tensor_tensor(a, y, y, ALU.mult))
                    yield
                    L.wait(n)
                    n = L.send(v.scalar_tensor_tensor(b, a, -0.5, x, ALU.mult, ALU.mult))
                    yield
                    L.wait(n)
                    n = L.send(v.scalar_tensor_tensor(r2 if turn == 2 else y, b, 1.5, y, ALU.add, ALU.mult))
                yield
                L.wait(n)
                v.scalar_tensor_tensor(mr2, mv2[:, :, 0], -1.0, r2, ALU.mult, ALU.mult).then_inc(done, 1)

            def scale_cell(t, par):
                dve.wait_ge(rb_mm, t + 1)
                v.tensor_tensor(cn, cell[par], PS[:, 4:6, :], ALU.mult).then_inc(cn_ready, 1)

            def hidden(t, par):
                dve.wait_ge(tanh_ready, t + 1)
                v.scalar_tensor_tensor(hT, g_o[par], 1.0, cn, ALU.add, ALU.mult).then_inc(h_ready, 1)

            JK = [P, BT, TOPK, E]

            def choose(t, par):
                dve.wait_ge(log_mm, t + 1)
                L(v.tensor_tensor(logit, PS[:, 7, 0:BT * E].rearrange("p (j e) -> p j e", e=E),
                                  bR.unsqueeze(1).to_broadcast([P, BT, E]), ALU.add), True)
                for j in range(BT):
                    last = v.max(top[:, j, :], logit[:, j, :])
                L(last, True)
                for j in range(BT):
                    last = v.max_index(topi[:, j, :], top[:, j, :], logit[:, j, :])
                L(last)
                v.tensor_tensor(wexp, top[:, :, 0:TOPK], top[:, :, 0:1].to_broadcast([P, BT, TOPK]),
                                ALU.subtract).then_inc(wdiff, 1)
                L(v.tensor_copy(topf, topi[:, :, 0:TOPK]))
                L(v.tensor_tensor(oh[:, :, :, :], K[:, C_IOTA:C_IOTA + E].unsqueeze(1).unsqueeze(1).to_broadcast(JK),
                                  topf.unsqueeze(3).to_broadcast(JK), ALU.is_equal))
                with nc.allow_low_precision("counts up to four are exact in bfloat16"):
                    v.tensor_reduce(chosen[:, :, :], oh[:, :, :, :].rearrange("p j k e -> p j e k"), AX,
                                    ALU.add).then_inc(chosen_ready, 1)

            def row_tails(t, par):
                def product(src):
                    return L.send(v.tensor_tensor(prod[:, :, :, :], oh[:, :, :, :], src.unsqueeze(3).to_broadcast(JK),
                                                  ALU.mult))

                def total(o):
                    return L.send(v.tensor_reduce(o, prod[:, :, :, :].rearrange("p j k e -> p j e k"), AX, ALU.add))

                Wb = Wd[:, ds(BT * t, BT), :]
                n = product(dest)
                dve.wait_ge(wexp_ready, t + 1)
                m = L.send(v.tensor_reduce(wsum, wexp, AX, ALU.add))
                yield
                L.wait(m)
                total(rows[par][:, :, DIM:DIM + E])
                m = L.send(v.reciprocal(wsum, wsum))
                yield
                L.wait(m)
                L.send(v.tensor_scalar(dest, dest, float(TOPK * BLK), None, ALU.add))
                n = L.send(v.tensor_tensor(wexp, wexp, wsum.unsqueeze(2).to_broadcast([P, BT, TOPK]), ALU.mult))
                yield
                L.wait(n)
                n = product(wexp)
                yield
                L.wait(n)
                n = total(Wb)
                yield
                L.wait(n)
                n = L.send(v.tensor_scalar(rows[par][:, :, DIM + E:ROW], Wb, 0.5, None, ALU.mult))
                yield
                L.wait(n)

            def slots(t, par):
                dve.wait_ge(rank_mm, t + 1)
                L(v.tensor_tensor(slot_e[:, :, :], PS[:, 7, 256:256 + BT * E].rearrange("p (j e) -> p j e", e=E),
                                  K[:, C_BASE:C_BASE + E].unsqueeze(1).to_broadcast([P, BT, E]), ALU.add))
                L(v.tensor_tensor(prod[:, :, :, :], oh[:, :, :, :],
                                  slot_e[:, :, :].unsqueeze(2).to_broadcast(JK), ALU.mult))
                L(v.tensor_reduce(slotf, prod[:, :, :, :], AX, ALU.add))
                v.tensor_copy(slot[par].rearrange("p (j k) -> p j k", k=TOPK), slotf).then_inc(slot_ready, 1)
                L(v.tensor_reduce(mstep[:, :], chosen[:, :, :].rearrange("p j e -> p e j"), AX, ALU.add))
                v.tensor_tensor(before[:, :], before[:, :], mstep[:, :], ALU.add).then_inc(before_ready, 1)

            def alternate(one, other):
                chains = [one, other]
                while chains:
                    for chain in list(chains):
                        if next(chain, "end") == "end":
                            chains.remove(chain)

            def scales(which):
                lo, hi = ((0, PARTS_GU), (PARTS_GU, PARTS))[which]
                dve.wait_ge(squared, hi + 1)
                L(v.tensor_reduce(peak, ssq[:, lo:hi], AX, ALU.max))
                v.tensor_copy(spread[which], peak.to_broadcast([P, P])).then_inc(peak_ready, 1)
                dve.wait_ge(peak_mm, which + 1)
                L(v.tensor_reduce(peak_all, PS[:, 2, which * P:(which + 1) * P], AX, ALU.max))
                L(v.tensor_scalar(expo, peak_all.bitcast(i32), 23, None, ALU.logical_shift_right))
                L(v.tensor_scalar(expo, expo, 1, None, ALU.add))
                L(v.tensor_scalar(expo, expo, 1, None, ALU.logical_shift_right))

                def power(o, sign, exponent):
                    return v.tensor_scalar(o.bitcast(i32), expo, sign * 2.0 ** 23, exponent * 2.0 ** 23, ALU.mult, ALU.add)

                if which == 0:
                    power(w_scale[0], -1, 205)
                    power(gu_inv, 1, 49 - X_BITS)
                    power(act_scale, 1, 49 - X_BITS + A_BITS)
                    L(power(gu_one, -1, 205 + X_BITS))
                    v.tensor_scalar(gu_lo, gu_one, -LIMIT, None, ALU.mult)
                    L(v.tensor_scalar(gu_hi, gu_one, LIMIT, None, ALU.mult))
                else:
                    power(w_scale[1], -1, 205)
                    L(power(y_inv, 1, 49 - A_BITS))
                dve.sem_inc(scale_ready, 1)

            def low(c, down):
                dve.wait_ge(high_done, c + 1)
                dve.nop(nofuse=True)
                hi, lo = halves(c, down)
                v.scalar_tensor_tensor(lo, source(c).rearrange("p (e x) -> p e x", e=2 if down else 1), w_scale[down],
                                       hi, ALU.mult, ALU.subtract).then_inc(low_done, 1)

            def bias_parts():
                rest, mid_part = bias_rest[:, 0:2 * FF], bias_rest[:, 2 * FF:3 * FF].bitcast(bf16)
                dve.wait_ge(bias_in, 48)
                yield L(v.tensor_scalar(bias_src[:, :], bias_src[:, :], gu_one, None, ALU.mult))
                yield L(v.tensor_copy(bias_gu[:, :], bias_src[:, :]))
                yield L(v.tensor_tensor(rest, bias_src[:, :], bias_gu[:, :], ALU.subtract))
                v.tensor_copy(bias_gu[32:64, :], rest[32:64, :])
                yield L(v.tensor_copy(mid_part, rest))
                yield L(v.tensor_tensor(rest, rest, mid_part, ALU.subtract))
                yield v.tensor_copy(bias_gu[64:96, :], rest[64:96, :]).then_inc(bias_done, 1)

            def step(s, s0, i=None):
                mid, old = on(s0, 1), on(s0, 2)
                pm, po = (s0 - 1) % 2, s0 % 2
                if mid:
                    scan(s - 1, pm)
                if s0 == 1:
                    norms_x(2 * BT, NTILE)
                if old:
                    residual(s - 2)
                if mid or old:
                    block_norms(s - 1, mid, old)
                if on(s0, 3):
                    list(row_tails(s - 3, pm))
                if s0 == NBLK:
                    dve.wait_ge(xT_mm, KT * NBLK)
                    v.memset(bias_src, 0.0).then_inc(bias_zero, 1)
                    scales(0)
                if s0 == NBLK + 1:
                    slots(s - 3, pm)
                    for c in range(3, EARLY_SPLIT - 2):
                        low(c, 0)
                if mid:
                    scale_cell(s - 1, pm)
                    if on(s0, 3):
                        slots(s - 3, pm)
                    hidden(s - 1, pm)
                if old:
                    choose(s - 2, po)
                if s0 == NBLK:
                    for c in range(2):
                        low(c, 0)
                if mid:
                    y_stats(s - 1)
                if mid:
                    list(y_norm())
                if s0 == NBLK:
                    low(2, 0)
                if s0 == NBLK + 1:
                    list(row_tails(s - 2, po))
                    slots(s - 2, po)

            steps(dve, step, L, PER_TURN)

            dve.wait_ge(cnt_mm, 1)
            L(v.tensor_tensor(tab_pad[:, :], PS[0:1, 0, 0:E], K[0:1, C_BASE:C_BASE + E], ALU.add))
            L(v.tensor_scalar(cnt_i, PS[0:E, 1, 0:1], float(P - 1), None, ALU.add))
            L(v.tensor_scalar(cnt_i, cnt_i, 7, None, ALU.logical_shift_right))
            L(v.tensor_copy(nt_col, cnt_i))
            v.tensor_scalar(dl_col, nt_col, -float(P), float(REGION), ALU.mult, ALU.add).then_inc(nt_ready, 1)
            low(EARLY_SPLIT - 2, 0)
            dve.wait_ge(end_mm, 1)
            L(v.tensor_copy(end_col, PS[0:E, 2, 0:1]))
            v.tensor_scalar(ended, K[0:E, C_TILE:C_TILE + TILES], end_col, None, ALU.is_ge).then_inc(cmp_ready, 1)
            low(EARLY_SPLIT - 1, 0)
            dve.wait_ge(tab_mm, 1)
            L(v.scalar_tensor_tensor(rowf, K[0:1, C_TILE:C_TILE + TILES], float(P), PS[0:1, 4, 0:TILES],
                                     ALU.mult, ALU.add))
            L(v.tensor_scalar(tab_row[:, :], rowf, float(PAD0), None, ALU.min))
            v.tensor_scalar(tab_e[:, :], PS[0:1, 3, 0:TILES], float(E - 1), None, ALU.min).then_inc(tab_ready, 1)

            scales(1)
            parts = bias_parts()
            for c in range(EARLY_SPLIT, PARTS_GU):
                low(c, 0)
                next(parts, None)
            with dve.Fori(0, PARTS_DN // 4) as i:
                for n in range(PARTS_GU, PARTS_GU + 4):
                    low(4 * i + n, 1)

            def x_low(j, uj):
                dve.wait_ge(xh_ready, j + 1)
                v.scalar_tensor_tensor(xl[uj % 2], PS[:, uj % 2, 0:DIM].rearrange("p (k t) -> p k t", k=KT),
                                       float(2 ** X_BITS), xh[uj % 2], ALU.mult, ALU.subtract).then_inc(xl_ready, 1)

            def a_low(j, uj):
                dve.wait_ge(ah_ready, j + 1)
                v.scalar_tensor_tensor(al[uj % 2], PS[:, 4 + uj % 2, 0:FF].rearrange("p (k t) -> p k t", k=KT),
                                       act_scale, ah[uj % 2], ALU.mult, ALU.subtract).then_inc(al_ready, 1)

            def tile_step(j, uj, i=None):
                running = i is not None
                b = uj % 2
                if uj == 0:
                    x_low(0, 0)
                    x_low(1, 1)
                if running or j < TILES:
                    dve.wait_ge(gu_mm, j + 1)
                    v.tensor_scalar(gate[b], PS[:, 2 + b, 0:FF], gu_inv, LIMIT, ALU.mult, ALU.min).then_inc(gate_ready, 1)
                    L.send(v.tensor_scalar(up[b], PS[:, 2 + b, FF:2 * FF], gu_hi, gu_lo, ALU.min, ALU.max))
                if running or j + 2 < TILES:
                    x_low(j + 2, uj + 2)
                if running or j < TILES:
                    dve.wait_ge(sg_ready, j + 1)
                    L(v.scalar_tensor_tensor(glu[b], sg[b], 1.0, gate[b], ALU.add, ALU.mult))
                    v.scalar_tensor_tensor(act_[b], up[b], gu_one, glu[b], ALU.add, ALU.mult).then_inc(act_ready, 1)
                if uj >= 1 and (running or j - 1 < TILES):
                    a_low(j - 1, uj - 1)

            tiles(dve, tile_step, L, 2 * UN)

            def sum_pairs(g, b, h):
                dve.wait_ge(zs_ready, BT * g + (2 * h + 2))
                dve.nop(nofuse=True)
                dve.wait_ge(zz_free, 2 * g + (h + 3))
                v.tensor_tensor(zz[h], zs[2 * b + h][:, :, 0, :], zs[2 * b + h][:, :, 1, :],
                                ALU.add).then_inc(zz_ready, 1)

            def add_z(g, b):
                dve.wait_ge(yz_ready, g + 3)
                for u in range(BT):
                    Xu = X[:, ds(BT * g + u, 1), :]
                    last = v.tensor_tensor(Xu, Xu, yz[b][:, u:u + 1, :], ALU.add)
                    if u < BT - 1:
                        yield
                last.then_inc(yo_ready, 1)

            def group(g, b, first=False, last=False):
                def rest():
                    if not last:
                        for h in range(2):
                            sum_pairs(g + 1, 1 - b, h)
                            yield
                    if not first:
                        yield from add_z(g - 1, 1 - b)

                dve.wait_ge(zz_free, 2 * g + 6)
                stats(lambda j: PS[:, 2 + 2 * b + j // 2, (j % 2) * DIM:(j % 2 + 1) * DIM], mv2, LN_EPS)
                alternate(y_norm(rz_ready), rest())

            for h in range(2):
                sum_pairs(0, 0, h)
            group(0, 0, first=True)
            with dve.Fori(0, NBLK // 2 - 1) as i:
                L.start(i, 28)
                group(2 * i + 1, 1)
                group(2 * i + 2, 0)
            L.stop(NBLK // 2 - 1)
            group(NBLK - 1, 1, last=True)
            list(add_z(NBLK - 1, 1))


def kernel(**inputs):
    import concourse.bacc as bacc
    from concourse.bass_utils import run_bass_kernel_spmd

    a = {n: np.asarray(inputs[n]) for n in inputs}

    def tiles_of(w):
        return np.ascontiguousarray(w.reshape(-1, P, w.shape[-1]).transpose(1, 0, 2))

    order = (3, 0, 1, 2)
    wg = a["L0_attn_W_gate"].reshape(PAIRS, 2, 4, HD, DIM)[:, :, order].transpose(2, 0, 1, 3, 4).reshape(GATES, DIM)
    bg = a["L0_attn_b_gate"].reshape(PAIRS, 2, 4, HD)[:, :, order].transpose(2, 0, 1, 3).reshape(CHUNKS, P)
    gu = a["L0_ffn_gate_up_proj"].reshape(E, KT, P, FF, 2).transpose(2, 0, 1, 4, 3)
    dn = a["L0_ffn_down_proj"].reshape(E, KT, P, DIM).transpose(2, 0, 1, 3)
    cst, cstb = constants()
    arrays = {
        "x": np.ascontiguousarray(a["L0_attn_x"].reshape(TOKENS, DIM)),
        "w_in": tiles_of(a["L0_attn_W_in"]),
        "w_gate": tiles_of(wg.T),
        "b_gate": np.ascontiguousarray(bg.T),
        "rms_w": np.ascontiguousarray(np.tile(a["L0_attn_rms_w"], 2).reshape(P, 1)),
        "w_out": tiles_of(a["L0_attn_W_out"].T),
        "w_router": tiles_of(a["L0_ffn_router_weight"].T),
        "b_router": np.ascontiguousarray(np.broadcast_to(a["L0_ffn_router_bias"], (P, E))),
        "w_gu": np.ascontiguousarray(gu).reshape(P, -1),
        "b_gu": np.ascontiguousarray(a["L0_ffn_gate_up_proj_bias"].reshape(E, FF, 2).transpose(0, 2, 1)).reshape(E, 2 * FF),
        "w_dn": np.ascontiguousarray(dn).reshape(P, -1),
        "b_dn": np.ascontiguousarray(a["L0_ffn_down_proj_bias"]),
        "cst": cst,
        "cstb": cstb,
    }
    nc = bacc.Bacc("TRN2", target_bir_lowering=False, num_devices=1)
    f32 = mybir.dt.float32
    args = [nc.dram_tensor(n, v.shape, f32, kind="ExternalInput").ap() for n, v in arrays.items()]
    out = nc.dram_tensor("out", [TOKENS, DIM], f32, kind="ExternalOutput").ap()
    build(nc, *args, out)
    r = run_bass_kernel_spmd(nc, [arrays], core_ids=[0])
    return r.results[0]["out"].reshape(BATCH, SEQ, DIM)
```
